# Optimizing a Trainium2 kernel written in Bass

```python
import numpy as np
import jax
import jax.numpy as jnp

def _softmax(x, axis=-1):
    return jax.nn.softmax(x, axis=axis)

def _gelu(x):
    return jax.nn.gelu(x, approximate=True)

def _silu(x):
    return jax.nn.silu(x)

def _sigmoid(x):
    return jax.nn.sigmoid(x)

def _layernorm(x, axis=-1, eps=1e-05):
    m = jnp.mean(x, axis=axis, keepdims=True)
    v = jnp.var(x, axis=axis, keepdims=True)
    return (x - m) / jnp.sqrt(v + eps)

def _scatter_add(tgt, idx, src, axis=0):
    return tgt.at[idx].add(src)

def _segment_sum(src, seg, n):
    return jax.ops.segment_sum(src, seg, n)
kernel_name = 'mk_gnn_preln_d2_gnn_r8_0c4fcf'

def setup_inputs(seed: int=0):
    np.random.seed(seed)
    _w = jnp.asarray

    def _rec_inputs():
        import jax
        import jax.numpy as jnp
        _gk = jax.random.key(seed)
        x = -0.0003713 + 1 * jax.random.normal(jax.random.fold_in(_gk, 1), (12500, 128), jnp.float32)
        src = jax.random.randint(jax.random.fold_in(_gk, 2), (400000,), 0, 12500, jnp.int32)
        dst = jnp.minimum((12500 * jax.random.uniform(jax.random.fold_in(_gk, 3), (400000,)) ** 2.0).astype(jnp.int32), 99999)
        _o = jnp.argsort(dst, stable=True)
        src = src[_o]
        dst = dst[_o]
        edge_attr_3 = -0.000451519 + 1.00018 * jax.random.normal(jax.random.fold_in(_gk, 12), (400000, 3), jnp.float32)
        edge_weight = jax.random.uniform(jax.random.fold_in(_gk, 14), (400000,), jnp.float32, 0.0, 0.999998)
        return (x, src, dst, edge_attr_3, edge_weight)
    x, src, dst, edge_attr_3, edge_weight = _rec_inputs()

    def _L0_gnn_setup():
        import jax, jax.numpy as jnp
        import numpy as np
        N_NODES = 12500
        N_EDGES = 200000
        D = 128

        def _sage_conv(h, src, dst, W_l, W_r, b, num_nodes):
            msg = h[src]
            agg = jax.ops.segment_sum(msg, dst, num_segments=num_nodes)
            deg = jax.ops.segment_sum(jnp.ones_like(dst, dtype=h.dtype), dst, num_segments=num_nodes)
            agg = agg / jnp.maximum(deg, 1.0)[:, None]
            return agg @ W_l + h @ W_r + b
        key = jax.random.key(seed)
        ks = jax.random.split(key, 8)
        scale = 1.0 / np.sqrt(D)
        x = jax.random.normal(ks[0], (N_NODES, D), dtype=jnp.float32)
        edge_index = jax.random.randint(ks[1], (2, N_EDGES), 0, N_NODES, dtype=jnp.int32)
        W1_l = jax.random.normal(ks[2], (D, D), dtype=jnp.float32) * scale
        W1_r = jax.random.normal(ks[3], (D, D), dtype=jnp.float32) * scale
        b1 = jnp.zeros((D,), dtype=jnp.float32)
        W2_l = jax.random.normal(ks[4], (D, D), dtype=jnp.float32) * scale
        W2_r = jax.random.normal(ks[5], (D, D), dtype=jnp.float32) * scale
        b2 = jnp.zeros((D,), dtype=jnp.float32)
        return {'x': x, 'edge_index': edge_index, 'W1_l': W1_l, 'W1_r': W1_r, 'b1': b1, 'W2_l': W2_l, 'W2_r': W2_r, 'b2': b2}
    _L0_gnn_all = _L0_gnn_setup()
    _L0_gnn_in = {k: v for k, v in _L0_gnn_all.items() if k in ('W1_l', 'W1_r', 'b1', 'W2_l', 'W2_r', 'b2')}
    del _L0_gnn_all

    def _L1_gnn_setup():
        import jax, jax.numpy as jnp
        import numpy as np
        N = 6250
        E = 100000
        MUL = 32
        NB = 8
        R_MAX = 1.0
        AVG = 16.0
        SQ3 = 3.0 ** 0.5

        def _radial_embedding(r):
            x = jnp.clip(r / R_MAX, 0.0, 1.0)
            centers = jnp.arange(NB, dtype=jnp.float32) / (NB - 1)
            sigma = 1.0 / (NB - 1)
            emb = jnp.exp(-0.5 * ((x[:, None] - centers[None, :]) / sigma) ** 2)
            emb = emb * NB ** 0.5 * (r <= R_MAX).astype(jnp.float32)[:, None]
            return emb
        key = jax.random.key(seed)
        k = jax.random.split(key, 12)
        inp = {'node_feats': jax.random.normal(k[0], (N, 4 * MUL), dtype=jnp.float32), 'edge_vec': jax.random.normal(k[1], (E, 3), dtype=jnp.float32), 'edge_length': jax.random.uniform(k[2], (E,), dtype=jnp.float32), 'senders': jax.random.randint(k[3], (E,), 0, N, dtype=jnp.int32), 'receivers': jax.random.randint(k[4], (E,), 0, N, dtype=jnp.int32), 'num_nodes': N, 'W_up0': jax.random.normal(k[5], (MUL, MUL), dtype=jnp.float32), 'W_up1': jax.random.normal(k[6], (MUL, MUL), dtype=jnp.float32), 'mlp_w0': jax.random.normal(k[7], (NB, 64), dtype=jnp.float32) / NB ** 0.5, 'mlp_b0': jnp.zeros((64,), dtype=jnp.float32), 'mlp_w1': jax.random.normal(k[8], (64, 64), dtype=jnp.float32) / 8.0, 'mlp_b1': jnp.zeros((64,), dtype=jnp.float32), 'mlp_w2': jax.random.normal(k[9], (64, 4 * MUL), dtype=jnp.float32) / 8.0, 'mlp_b2': jnp.zeros((4 * MUL,), dtype=jnp.float32), 'W_out0': jax.random.normal(k[10], (2 * MUL, MUL), dtype=jnp.float32), 'W_out1': jax.random.normal(k[11], (2 * MUL, MUL), dtype=jnp.float32)}
        return inp
    _L1_gnn_all = _L1_gnn_setup()
    _L1_gnn_in = {k: v for k, v in _L1_gnn_all.items() if k in ('W_up0', 'W_up1', 'mlp_w0', 'mlp_b0', 'mlp_w1', 'mlp_b1', 'mlp_w2', 'mlp_b2', 'W_out0', 'W_out1')}
    del _L1_gnn_all
    return {'x': x, 'src': src, 'dst': dst, 'edge_attr_3': edge_attr_3, 'edge_weight': edge_weight, 'L0_gnn_W1_l': _L0_gnn_in['W1_l'], 'L0_gnn_W1_r': _L0_gnn_in['W1_r'], 'L0_gnn_b1': _L0_gnn_in['b1'], 'L0_gnn_W2_l': _L0_gnn_in['W2_l'], 'L0_gnn_W2_r': _L0_gnn_in['W2_r'], 'L0_gnn_b2': _L0_gnn_in['b2'], 'L1_gnn_W_up0': _L1_gnn_in['W_up0'], 'L1_gnn_W_up1': _L1_gnn_in['W_up1'], 'L1_gnn_mlp_w0': _L1_gnn_in['mlp_w0'], 'L1_gnn_mlp_b0': _L1_gnn_in['mlp_b0'], 'L1_gnn_mlp_w1': _L1_gnn_in['mlp_w1'], 'L1_gnn_mlp_b1': _L1_gnn_in['mlp_b1'], 'L1_gnn_mlp_w2': _L1_gnn_in['mlp_w2'], 'L1_gnn_mlp_b2': _L1_gnn_in['mlp_b2'], 'L1_gnn_W_out0': _L1_gnn_in['W_out0'], 'L1_gnn_W_out1': _L1_gnn_in['W_out1']}

def reference(x, src, dst, edge_attr_3, edge_weight, L0_gnn_W1_l, L0_gnn_W1_r, L0_gnn_b1, L0_gnn_W2_l, L0_gnn_W2_r, L0_gnn_b2, L1_gnn_W_up0, L1_gnn_W_up1, L1_gnn_mlp_w0, L1_gnn_mlp_b0, L1_gnn_mlp_w1, L1_gnn_mlp_b1, L1_gnn_mlp_w2, L1_gnn_mlp_b2, L1_gnn_W_out0, L1_gnn_W_out1):
    import jax
    import jax.numpy as jnp

    def _L0_gnn_ref(x, edge_index, W1_l, W1_r, b1, W2_l, W2_r, b2):
        import jax, jax.numpy as jnp
        import numpy as np
        N_NODES = 12500
        N_EDGES = 200000
        D = 128

        def _sage_conv(h, src, dst, W_l, W_r, b, num_nodes):
            msg = h[src]
            agg = jax.ops.segment_sum(msg, dst, num_segments=num_nodes)
            deg = jax.ops.segment_sum(jnp.ones_like(dst, dtype=h.dtype), dst, num_segments=num_nodes)
            agg = agg / jnp.maximum(deg, 1.0)[:, None]
            return agg @ W_l + h @ W_r + b
        num_nodes = x.shape[0]
        src, dst = (edge_index[0], edge_index[1])
        residual = x
        out = _sage_conv(x, src, dst, W1_l, W1_r, b1, num_nodes)
        out = jax.nn.relu(out)
        out = _sage_conv(out, src, dst, W2_l, W2_r, b2, num_nodes)
        return out + residual

    def _L1_gnn_ref(node_feats, edge_vec, edge_length, senders, receivers, num_nodes, W_up0, W_up1, mlp_w0, mlp_b0, mlp_w1, mlp_b1, mlp_w2, mlp_b2, W_out0, W_out1):
        import jax, jax.numpy as jnp
        import numpy as np
        N = 6250
        E = 100000
        MUL = 32
        NB = 8
        R_MAX = 1.0
        AVG = 16.0
        SQ3 = 3.0 ** 0.5

        def _radial_embedding(r):
            x = jnp.clip(r / R_MAX, 0.0, 1.0)
            centers = jnp.arange(NB, dtype=jnp.float32) / (NB - 1)
            sigma = 1.0 / (NB - 1)
            emb = jnp.exp(-0.5 * ((x[:, None] - centers[None, :]) / sigma) ** 2)
            emb = emb * NB ** 0.5 * (r <= R_MAX).astype(jnp.float32)[:, None]
            return emb
        f32 = jnp.float32
        rhat = edge_vec / (jnp.linalg.norm(edge_vec, axis=-1, keepdims=True) + 1e-12)
        Y1 = SQ3 * rhat
        emb = _radial_embedding(edge_length)
        h = jax.nn.silu(emb @ mlp_w0 + mlp_b0)
        h = jax.nn.silu(h @ mlp_w1 + mlp_b1)
        w = (h @ mlp_w2 + mlp_b2).reshape(-1, 4, MUL)
        s = node_feats[:, :MUL]
        v = node_feats[:, MUL:].reshape(-1, MUL, 3)
        xs = s @ W_up0 / f32(MUL) ** 0.5
        xv = jnp.einsum('nmc,mk->nkc', v, W_up1) / f32(MUL) ** 0.5
        ss = xs[senders]
        vv = xv[senders]
        m0 = w[:, 0] * ss
        m1 = w[:, 1][:, :, None] * ss[:, :, None] * Y1[:, None, :]
        m2 = w[:, 2][:, :, None] * vv
        m3 = w[:, 3] * (jnp.einsum('emc,ec->em', vv, Y1) / SQ3)
        mid_s = jnp.concatenate([m0, m3], axis=1)
        mid_v = jnp.concatenate([m1, m2], axis=1)
        msg_s = jax.ops.segment_sum(mid_s, receivers, num_segments=num_nodes)
        msg_v = jax.ops.segment_sum(mid_v, receivers, num_segments=num_nodes)
        out_s = msg_s @ W_out0 / f32(2 * MUL) ** 0.5
        out_v = jnp.einsum('nmc,mk->nkc', msg_v, W_out1) / f32(2 * MUL) ** 0.5
        out = jnp.concatenate([out_s, out_v.reshape(-1, 3 * MUL)], axis=1)
        return out / max(AVG, 1e-08)
    edge_index = jnp.stack([src, dst])
    h = jnp.maximum(_layernorm(x, axis=-1), 0.0)
    x = x + _L0_gnn_ref(h, edge_index, L0_gnn_W1_l, L0_gnn_W1_r, L0_gnn_b1, L0_gnn_W2_l, L0_gnn_W2_r, L0_gnn_b2)
    h = jnp.maximum(_layernorm(x, axis=-1), 0.0)
    x = x + _L1_gnn_ref(h, edge_attr_3, edge_weight, src, dst, 12500, L1_gnn_W_up0, L1_gnn_W_up1, L1_gnn_mlp_w0, L1_gnn_mlp_b0, L1_gnn_mlp_w1, L1_gnn_mlp_b1, L1_gnn_mlp_w2, L1_gnn_mlp_b2, L1_gnn_W_out0, L1_gnn_W_out1)
    return x

_drawn_inputs = setup_inputs


def setup_inputs(seed=0):
    import zlib

    import numpy as np

    out = dict(_drawn_inputs(seed))
    spreads = {'L0_gnn_b1': (0.0, 0.1),
     'L0_gnn_b2': (0.0, 0.1),
     'L1_gnn_mlp_b0': (0.0, 0.362),
     'L1_gnn_mlp_b1': (0.0, 0.1),
     'L1_gnn_mlp_b2': (0.0, 0.1)}
    factors = {}
    for name, (base, spread) in spreads.items():
        noise = np.random.default_rng([zlib.crc32(name.encode()), seed]).standard_normal(out[name].shape)
        drawn = base * np.exp(spread * noise) if base else spread * noise
        out[name] = jnp.asarray(drawn.astype(out[name].dtype))
    for name, factor in factors.items():
        out[name] = (out[name] * factor).astype(out[name].dtype)
    return out
```

```python
import math
from contextlib import ExitStack

import concourse.bass as bass
from concourse import mybir

F32 = mybir.dt.float32
I32 = mybir.dt.int32
ALU = mybir.AluOpType
ACT = mybir.ActivationFunctionType
AX = mybir.AxisListType
ds = bass.ds

P = 128
T = 5
S = 5
W = 64
GE = P * T
ST = S * T
NR, NK = 125, 4
CH = NR * NK
D = 128
MUL = 32
NB = 8
HID = 64
PAIRS = (T + 1) // 2
LN_EPS = 1e-5
AVG = 16.0


class Signals:

    def __init__(self, nc, ctx):
        self.nc, self.ctx, self.made = nc, ctx, []

    def one(self, name):
        s = self.ctx.enter_context(self.nc.semaphore(name))
        self.made.append(s)
        return s

    def some(self, *names):
        return [self.one(n) for n in names]

    def slots(self, name):
        return [self.one(f"{name}{q}") for q in range(S)]

    def clear(self):
        for r in runs(self.made):
            self.nc.all_engine_barrier(sems_to_clear=r)


def runs(semaphores):
    numbers = sorted(s.num for s in semaphores)
    starts = [n for n in numbers if n - 1 not in numbers]
    ends = [n + 1 for n in numbers if n + 1 not in numbers]
    return [range(a, b) for a, b in zip(starts, ends)]


def sig_reset(pool, semaphores):
    for r in runs(semaphores):
        pool.dma_reset(r)




def spread(ap, shape):
    return ap.broadcast_to(list(shape))


def program(nc, x, src, dst, attr, weight, w1l, w1r, b1, w2l, w2r, b2, up0, up1,
            m0, mb0, m1, mb1, m2, mb2, wo0, wo1, out):
    N = x.shape[0]
    E = src.shape[0]
    GROUPS = E // GE
    ITERS = GROUPS // S
    CHUNKS = N // CH
    CITERS = CHUNKS // S
    GP = GROUPS // S
    assert GROUPS * GE == E and ITERS * S == GROUPS and CHUNKS * CH == N and CITERS * S == CHUNKS
    assert GP <= P

    def table(name, shape, dt=F32):
        return nc.dram_tensor(name, shape, dt, kind="Internal").ap()

    h_tab, o_tab, x2_tab, up_tab = (table(n, [N, D]) for n in ("h_tab", "o_tab", "x2_tab", "up_tab"))
    base_tab = table("base_tab", [1, GROUPS], I32)
    dir_tab = table("dir_tab", [GROUPS, P, T * 3])
    emb_tab = table("emb_tab", [GROUPS, T * NB, P])
    weight_tab = table("weight_tab", [GROUPS, P, T * D])

    src_v = src.rearrange("(g p t) -> g p t", p=P, t=T)
    dst_v = dst.rearrange("(g p t) -> g p t", p=P, t=T)
    attr_v = attr.rearrange("(g p t) c -> g p (t c)", p=P, t=T)
    weight_v = weight.rearrange("(g p t) -> g p t", p=P, t=T)

    def group_of(view, g):
        return view[ds(g, 1)].rearrange("g p n -> (g p) n")

    def chunk_of(tab, c):
        return tab.rearrange("(c p k) d -> c p k d", p=NR, k=NK)[ds(c, 1)].rearrange("c p k d -> (c p) k d")

    with ExitStack() as ctx:
        def sb(name, shape, dt=F32):
            return ctx.enter_context(nc.sbuf_tensor(name, shape, dt))

        agg = sb("agg", [P, 2, N + W])
        gathered = sb("gathered", [P, S, T * D])
        msgs = sb("msgs", [P, S, T * 2 * D])
        path_w = sb("path_w", [P, S, T * D])
        onehot = sb("onehot", [P, S, T, W])
        src_i = sb("src_i", [P, S, T], I32)
        dst_i = sb("dst_i", [P, S, T], I32)
        dirs = sb("dirs", [P, S, T * 3])
        embT = sb("embT", [T * NB, S, P])
        work = sb("work", [P, S, 512])
        slot_a = [gathered[0:NR, q, 0:512].rearrange("p (k d) -> p k d", k=NK) for q in range(S)]
        slot_b = [msgs[0:NR, q, 0:512].rearrange("p (k d) -> p k d", k=NK) for q in range(S)]
        slot_c = [msgs[0:NR, q, 512:1024].rearrange("p (k d) -> p k d", k=NK) for q in range(S)]
        slot_sum = [path_w[:, q, 0:CH] for q in range(S)]
        slot_t = [work[:, q, 0:CH] for q in range(S)]
        group_base = sb("group_base", [P, GROUPS])
        round_base = sb("round_base", [P, GROUPS])
        addr_i = sb("addr_i", [P, GROUPS], I32)
        span_i = sb("span_i", [1, 1], I32)
        extremes = sb("extremes", [P, 12])
        iota_w = sb("iota_w", [P, W])
        centres = sb("centres", [P, NB])
        ident, ones = sb("ident", [P, P]), sb("ones", [P, P])
        zeros = sb("zeros", [P, CH])
        eps = sb("eps", [P, 1])
        bn6, mean_var = sb("bn6", [P, S, NK, 6]), sb("mean_var", [P, S, NK, 2])
        rstd, shift = sb("rstd", [P, S, NK]), sb("shift", [P, S, NK])
        W1L, W1R, W2L, W2R, WUP, WOA, WOB = (sb(n, [D, D]) for n in ("W1L", "W1R", "W2L", "W2R", "WUP", "WOA", "WOB"))
        B1, B2 = sb("B1", [P, D]), sb("B2", [P, D])
        M0 = sb("M0", [T * NB, PAIRS, P])
        M1 = sb("M1", [P, P])
        M2 = sb("M2", [P, 2 * D])
        MB0, MB1 = sb("MB0", [P, 1]), sb("MB1", [P, 1])
        MB2 = sb("MB2", [P, D])
        stage = sb("stage", [P, 2, MUL])
        bank = [ctx.enter_context(nc.psum_tensor(f"bank{i}", [P, 512], F32)) for i in range(8)]

        with ExitStack() as phase:
            sig = Signals(nc, phase)
            dst_loaded, loaded, placed, staged, base_out, base_in = sig.some(
                "dst_loaded", "loaded", "placed", "staged", "base_out", "base_in")
            filled, ident_made, extremes_made, least_made, span_step, span_t, base_made = sig.some(
                "filled", "ident_made", "extremes_made", "least_made", "span_step", "span_t", "base_made")
            dst_rows = gathered[0:GP, :, :].rearrange("p s n -> p (s n)").bitcast(I32)
            least, most = extremes[0:GP, 0:S], extremes[0:GP, S:2 * S]
            least_i = src_i[0:GP, 0, :]
            OUT1 = [(WOA, 64, 0, 0), (WOB, 0, 1, 1), (WOB, 64, 1, 2)]

            with nc.Block() as block:
                @block.sync
                def _(sp):
                    sp.dma_start(dst_rows, dst.rearrange("(p n) -> p n", p=GP)).then_inc(dst_loaded, 16)
                    n = 0
                    for to, of in ((W1L, w1l), (W1R, w1r), (W2L, w2l), (W2R, w2r)):
                        sp.dma_start(to[:, :], of).then_inc(loaded, 16)
                        n += 1
                    for to, of in ((B1, b1), (B2, b2), (MB2, mb2)):
                        sp.dma_start(to[:, :], spread(of.rearrange("(a n) -> a n", a=1), [P, D])).then_inc(loaded, 16)
                        n += 1
                    for j in range(2):
                        for to, of in ((MB0, mb0), (MB1, mb1)):
                            sp.dma_start(to[HID * j:HID * (j + 1), :], of.rearrange("(n a) -> n a", a=1)).then_inc(loaded, 16)
                            n += 1
                    for _, row, a, _ in OUT1:
                        sp.dma_start(stage[row:row + 2 * MUL, a, :], wo1).then_inc(staged, 16)
                    sp.wait_ge(filled, 1)
                    blocks = [(WUP[0:MUL, 0:MUL], up0), (WOA[0:2 * MUL, 0:MUL], wo0)]
                    blocks += [(WUP[MUL + c:MUL + c + 3 * (MUL - 1) + 1:3, MUL * (1 + c):MUL * (2 + c)], up1) for c in range(3)]
                    blocks += [(M0[NB * t:NB * (t + 1), t // 2, HID * (t % 2):HID * (t % 2 + 1)], m0) for t in range(T)]
                    blocks += [(M1[HID * j:HID * (j + 1), HID * j:HID * (j + 1)], m1) for j in range(2)]
                    blocks += [(M2[HID * j:HID * (j + 1), D * j:D * (j + 1)], m2) for j in range(2)]
                    for to, of in blocks:
                        sp.dma_start(to, of).then_inc(placed, 16)
                    sp.wait_ge(least_made, 1)
                    sp.dma_start(base_tab.rearrange("a (p s) -> (a p) s", s=S), least_i).then_inc(base_out, 16)
                    sp.wait_ge(base_out, 16)
                    sp.dma_start(addr_i[:, :], spread(base_tab, [P, GROUPS])).then_inc(base_in, 16)
                    sp.wait_ge(loaded, 16 * n)
                    sp.wait_ge(placed, 16 * len(blocks))

                @block.gpsimd
                def _(pool):
                    for tile in (WUP, WOA, WOB, M1, M2, zeros, ident):
                        pool.memset(tile[:, :], 0.0)
                    pool.memset(M0[:, :, :], 0.0)
                    pool.memset(eps[:, :], LN_EPS)
                    pool.memset(ones[:, :], 1.0).then_inc(filled, 1)
                    pool.wait_ge(filled, 1)
                    pool.affine_select(out=ident[:, :], in_=ident[:, :], compare_op=ALU.not_equal, fill=1.0,
                                       base=0, pattern=[[-1, P]], channel_multiplier=1)
                    pool.iota(iota_w[:, :], [[1, W]], base=0, channel_multiplier=0,
                              allow_small_or_imprecise_dtypes=True).then_inc(ident_made, 1)

                @block.vector
                def _(dve):
                    dve.wait_ge(dst_loaded, 16)
                    rows = dst_rows.rearrange("p (s e) -> p s e", s=S)
                    nc.vector.tensor_reduce(least, rows, axis=AX.X, op=ALU.min).then_inc(extremes_made, 1)
                    nc.vector.tensor_reduce(most, rows, axis=AX.X, op=ALU.max).then_inc(extremes_made, 1)
                    dve.wait_ge(extremes_made, 2)
                    nc.vector.tensor_copy(least_i, least).then_inc(least_made, 1)
                    nc.vector.tensor_tensor(most, most, least, ALU.subtract).then_inc(span_step, 1)
                    dve.wait_ge(span_step, 1)
                    nc.vector.tensor_reduce(extremes[0:GP, 10:11], most, axis=AX.X, op=ALU.max).then_inc(span_step, 1)
                    dve.wait_ge(span_t, 1)
                    nc.vector.tensor_reduce(extremes[0:1, 11:12], bank[0][0:1, 0:GP], axis=AX.X, op=ALU.max).then_inc(span_step, 1)
                    dve.wait_ge(span_step, 3)
                    nc.vector.tensor_copy(span_i[:, :], extremes[0:1, 11:12])
                    dve.wait_ge(ident_made, 1)
                    nc.vector.tensor_scalar(centres[:, :], iota_w[:, 0:NB], 1.0 / (NB - 1), None, ALU.mult)
                    for k in range(2):
                        nc.vector.memset(agg[:, k, :], 0.0)
                    dve.wait_ge(staged, 48)
                    for to, row, a, c in OUT1:
                        nc.vector.tensor_copy(to[row:row + 2 * MUL, MUL + c:MUL + c + 3 * (MUL - 1) + 1:3], stage[row:row + 2 * MUL, a, :])
                    dve.wait_ge(base_in, 16)
                    nc.vector.tensor_copy(group_base[:, :], addr_i[:, :])

                @block.tensor
                def _(pe):
                    pe.wait_ge(ident_made, 1)
                    pe.wait_ge(span_step, 2)
                    nc.tensor.transpose(bank[0][0:1, 0:GP], extremes[0:GP, 10:11], ident[0:GP, 0:GP]).then_inc(span_t, 1)
            sig.clear()

        span = nc.values_load(span_i[0:1, 0:1], min_val=0, max_val=N - 1)

        def row_stats(dve, q, rows, s, stats_made, var_made, std_made, inverted, scales_made, waited):
            for k in range(NK):
                last = nc.vector.bn_stats(bn6[0:NR, q, k, :], rows[:, k, :])
            last.then_inc(stats_made, 1)
            dve.wait_ge(stats_made, s)
            dve.sem_inc(waited, 1)
            for k in range(NK):
                last = nc.vector.bn_aggr(mean_var[0:NR, q, k, :], bn6[0:NR, q, k, :])
            last.then_inc(var_made, 1)
            dve.wait_ge(std_made, s)
            nc.vector.reciprocal(rstd[0:NR, q, :], rstd[0:NR, q, :]).then_inc(inverted, 1)
            dve.wait_ge(inverted, s)
            nc.vector.scalar_tensor_tensor(out=shift[0:NR, q, :], in0=mean_var[0:NR, q, :, 0], scalar=-1.0,
                                           in1=rstd[0:NR, q, :], op0=ALU.mult, op1=ALU.mult).then_inc(scales_made, 1)

        def row_std(q):
            return nc.scalar.activation(rstd[0:NR, q, :], mean_var[0:NR, q, :, 1], ACT.Sqrt, bias=eps[0:NR, :])

        def norm_relu(q, to, rows):
            for k in range(NK):
                last = nc.scalar.activation(to[:, k, :], rows[:, k, :], ACT.Relu,
                                            bias=shift[0:NR, q, k:k + 1], scale=rstd[0:NR, q, k:k + 1])
            return last

        def to_features(q, rows):
            for k in range(NK):
                last = nc.tensor.transpose(bank[q % 2][:, NR * k:NR * (k + 1)], rows[:, k, :], ident[0:NR, 0:NR])
            return last

        def row_matmuls(to, terms):
            for k in range(NK):
                for i, (cols, weights) in enumerate(terms):
                    last = nc.tensor.matmul(to[0:NR, D * k:D * (k + 1)], cols(k), weights[:, :],
                                            start=(i == 0), stop=(i == len(terms) - 1))
            return last

        def strided(tile):
            return lambda k: tile[:, k:k + NK * (NR - 1) + 1:NK]

        def packed(tile):
            return lambda k: tile[:, NR * k:NR * (k + 1)]

        def rows_of(psum):
            return psum[0:NR, :].rearrange("p (k d) -> p k d", k=NK)

        def store_chunks(pool, tab, slots, made, stored, free, waited):
            with pool.Fori(0, CITERS) as it:
                for q in range(S):
                    pool.wait_ge(made, it * S + (q + 1 + S))
                    pool.sem_inc(waited, 1)
                    pool.dma_start(chunk_of(tab, it * S + q), slots[q]).then_inc(stored[q], 16)
                    if q >= 1:
                        pool.wait_ge(stored[q - 1], it * 16 + 16)
                        pool.sem_inc(free, 1)
                pool.wait_ge(stored[S - 1], it * 16 + 16)
                pool.sem_inc(free, 1)
            sig_reset(pool, stored)

        with ExitStack() as phase:
            sig = Signals(nc, phase)
            x_in, h_stored = sig.slots("x_in"), sig.slots("h_stored")
            waited, stats_made, var_made, std_made, inverted, scales_made, h_made = sig.some(
                "waited", "stats_made", "var_made", "std_made", "inverted", "scales_made", "h_made")
            h_free, pool_waited = sig.some("h_free", "pool_waited")
            with nc.Block() as block:
                @block.sync
                def _(sp):
                    sp.sem_inc(h_made, S)
                    with sp.Fori(0, CITERS) as it:
                        for q in range(S):
                            sp.wait_ge(h_made, it * S + (q + 1))
                            sp.dma_start(slot_a[q], chunk_of(x, it * S + q)).then_inc(x_in[q], 16)

                @block.vector
                def _(dve):
                    with dve.Fori(0, CITERS) as it:
                        for q in range(S):
                            dve.wait_ge(x_in[q], it * 16 + 16)
                            row_stats(dve, q, slot_a[q], it * S + (q + 1), stats_made, var_made, std_made, inverted, scales_made, waited)

                @block.scalar
                def _(act):
                    act.sem_inc(h_free, S)
                    with act.Fori(0, CITERS) as it:
                        for q in range(S):
                            act.wait_ge(var_made, it * S + (q + 1))
                            row_std(q).then_inc(std_made, 1)
                            act.wait_ge(scales_made, it * S + (q + 1))
                            act.wait_ge(h_free, it * S + (q + 1))
                            norm_relu(q, slot_b[q], slot_a[q]).then_inc(h_made, 1)

                @block.gpsimd
                def _(pool):
                    store_chunks(pool, h_tab, slot_b, h_made, h_stored, h_free, pool_waited)
            sig.clear()

        def start_rounds():
            with nc.Block() as block:
                @block.vector
                def _(dve):
                    nc.vector.tensor_scalar(round_base[:, :], group_base[:, :], float(-W), None, ALU.add)

        def move_windows(dve, moved, addressed):
            nc.vector.tensor_scalar(round_base[:, :], round_base[:, :], float(W), None, ALU.add).then_inc(moved, 1)
            dve.wait_ge(moved, 1)
            nc.vector.tensor_scalar(addr_i[0:1, :], round_base[0:1, :], float(N), None, ALU.min).then_inc(addressed, 1)
            dve.wait_ge(addressed, 1)

        def load_indices(sp, q, g, src_in, dst_in):
            sp.dma_start(src_i[:, q, :], group_of(src_v, g)).then_inc(src_in[q], 16)
            sp.dma_start(dst_i[:, q, :], group_of(dst_v, g)).then_inc(dst_in[q], 16)

        def gather_rows(pool, rows_of_table, src_in, rows_in, groups_begun):
            with pool.Fori(0, ITERS) as it:
                for q in range(S):
                    pool.wait_ge(src_in[q], it * 16 + 16)
                    pool.sem_inc(groups_begun, 1)
                    for t in range(T):
                        pool.indirect_dma_start(
                            out=gathered[:, q, D * t:D * (t + 1)], out_offset=None, in_=rows_of_table,
                            in_offset=bass.IndirectOffsetOnAxis(ap=src_i[:, q, t:t + 1], axis=0)).then_inc(rows_in[q], 16)
            for q in range(S):
                pool.wait_ge(rows_in[q], 16 * T * ITERS)
            sig_reset(pool, rows_in)

        def make_onehot(q, g):
            return nc.vector.scalar_tensor_tensor(
                out=onehot[:, q, :, :], in0=spread(dst_i[:, q, :].rearrange("p (t a) -> p t a", a=1), [P, T, W]),
                scalar=round_base[:, ds(g, 1)], in1=spread(iota_w[:, :].rearrange("p (a j) -> p a j", a=1), [P, T, W]),
                op0=ALU.subtract, op1=ALU.is_equal)

        def add_window(dve, g, halves, sums):
            at = dve.value_load(addr_i[0:1, ds(g, 1)], min_val=0, max_val=N)
            where = agg[:, 0:halves, ds(at, W)]
            return nc.vector.tensor_tensor(where, where, sums.rearrange("p (a j) -> p a j", a=halves), ALU.add)

        def along(ap, n):
            return spread(ap.rearrange("p (e a) -> p e a", a=1), [P, ap.shape[1], n])

        def first_pass():
            with ExitStack() as phase:
                sig = Signals(nc, phase)
                src_in, dst_in, rows_in = sig.slots("src_in"), sig.slots("dst_in"), sig.slots("rows_in")
                groups_begun = sig.one("groups_begun")
                moved, addressed, onehot_made, summed, window_added = sig.some(
                    "moved", "addressed", "onehot_made", "summed", "window_added")
                vec_in, squared, norm2_made, norm_made, norm_kept, norm_inverted, dirs_made, dirs_stored = sig.some(
                    "vec_in", "squared", "norm2_made", "norm_made", "norm_kept", "norm_inverted", "dirs_made", "dirs_stored")
                len_in, clipped, offset_made, square_made, gauss_made, emb_made, emb_turned, emb_ready, emb_stored = sig.some(
                    "len_in", "clipped", "offset_made", "square_made", "gauss_made", "emb_made", "emb_turned", "emb_ready", "emb_stored")
                vec, sq, made = (work[:, i, 0:ST * 3] for i in range(3))
                norm2, norm, kept, inverse, length, clip, inside = (work[:, 3, 32 * i:32 * i + ST] for i in range(7))
                offset, square, gauss, emb = (msgs[:, 1, 256 * i:256 * i + ST * NB] for i in range(4))
                turned = msgs[0:T * NB, 0, 0:S * P]
                turns = [(bank[5], 0, 4), (bank[6], 4, S)]

                def by_edge(ap, n):
                    return ap.rearrange("p (e c) -> p e c", c=n)

                def squared_norms(dve, it):
                    dve.wait_ge(vec_in, it * 16 + 16)
                    nc.vector.tensor_tensor(sq, vec, vec, ALU.mult).then_inc(squared, 1)
                    dve.wait_ge(squared, it + 1)
                    nc.vector.tensor_reduce(norm2, by_edge(sq, 3), axis=AX.X, op=ALU.add).then_inc(norm2_made, 1)

                def squared_offsets(dve, it):
                    dve.wait_ge(len_in, it * 16 + 16)
                    nc.vector.tensor_scalar(clip, length, 0.0, 1.0, ALU.max, ALU.min)
                    nc.vector.tensor_scalar(inside, length, 1.0, math.sqrt(NB), ALU.is_le, ALU.mult).then_inc(clipped, 1)
                    dve.wait_ge(clipped, it + 1)
                    nc.vector.tensor_tensor(by_edge(offset, NB), along(clip, NB),
                                            spread(centres[:, :].rearrange("p (a k) -> p a k", a=1), [P, ST, NB]),
                                            ALU.subtract).then_inc(offset_made, 1)
                    dve.wait_ge(offset_made, it + 1)
                    nc.vector.tensor_tensor(square, offset, offset, ALU.mult).then_inc(square_made, 1)

                def directions(dve, it):
                    dve.wait_ge(norm_made, it + 1)
                    nc.vector.tensor_scalar(kept, norm, 1e-12, None, ALU.add).then_inc(norm_kept, 1)
                    dve.wait_ge(norm_kept, it + 1)
                    nc.vector.reciprocal(inverse, kept).then_inc(norm_inverted, 1)
                    dve.wait_ge(norm_inverted, it + 1)
                    nc.vector.scalar_tensor_tensor(out=by_edge(made, 3), in0=by_edge(vec, 3), scalar=math.sqrt(3.0),
                                                   in1=along(inverse, 3), op0=ALU.mult, op1=ALU.mult).then_inc(dirs_made, 1)

                def embeddings(dve, it):
                    dve.wait_ge(gauss_made, it + 1)
                    nc.vector.tensor_tensor(by_edge(emb, NB), by_edge(gauss, NB), along(inside, NB), ALU.mult).then_inc(emb_made, 1)

                start_rounds()
                with nc.Fori(0, span + 1, W):
                    with nc.Block() as block:
                        @block.sync
                        def _(sp):
                            sp.sem_inc(dirs_made, 1)
                            sp.sem_inc(emb_made, 1)
                            with sp.Fori(0, ITERS) as it:
                                for q in range(S):
                                    sp.wait_ge(summed, it * S + (q + 1))
                                    load_indices(sp, q, it * S + q, src_in, dst_in)
                                    if q == 0:
                                        sp.wait_ge(dirs_made, it + 1)
                                        sp.dma_start(vec.rearrange("p (s n) -> p s n", s=S),
                                                     attr_v[ds(it * S, S)].rearrange("s p n -> p s n")).then_inc(vec_in, 16)
                                        sp.wait_ge(emb_made, it + 1)
                                        sp.dma_start(length.rearrange("p (s n) -> p s n", s=S),
                                                     weight_v[ds(it * S, S)].rearrange("s p n -> p s n")).then_inc(len_in, 16)

                        @block.gpsimd
                        def _(pool):
                            gather_rows(pool, h_tab, src_in, rows_in, groups_begun)

                        @block.tensor
                        def _(pe):
                            pe.sem_inc(summed, S)
                            with pe.Fori(0, ITERS) as it:
                                for q in range(S):
                                    pe.wait_ge(onehot_made, it * S + (q + 1))
                                    for t in range(T):
                                        nc.tensor.matmul(bank[q][:, W:2 * W], ones[:, :], onehot[:, q, t, :], start=(t == 0), stop=(t == T - 1))
                                    if q == S - 1:
                                        pe.wait_ge(emb_made, it + 2)
                                    pe.wait_ge(rows_in[q], it * 16 * T + 16 * T)
                                    for t in range(T):
                                        last = nc.tensor.matmul(bank[q][:, 0:W], gathered[:, q, D * t:D * (t + 1)], onehot[:, q, t, :],
                                                                start=(t == 0), stop=(t == T - 1))
                                    last.then_inc(summed, 1)
                                for to, a, b in turns:
                                    for j in range(a, b):
                                        last = nc.tensor.transpose(to[0:T * NB, P * (j - a):P * (j - a + 1)],
                                                                   emb[:, T * NB * j:T * NB * (j + 1)], ident[:, :])
                                last.then_inc(emb_turned, 1)

                        @block.scalar
                        def _(act):
                            with act.Fori(0, ITERS) as it:
                                act.wait_ge(norm2_made, it + 1)
                                nc.scalar.activation(norm, norm2, ACT.Sqrt).then_inc(norm_made, 1)
                                act.wait_ge(square_made, it + 1)
                                nc.scalar.activation(gauss, square, ACT.Exp, scale=-0.5 * (NB - 1) ** 2).then_inc(gauss_made, 1)
                                act.wait_ge(dirs_made, it + 2)
                                act.dma_start(dir_tab[ds(it * S, S)].rearrange("s p n -> p s n"),
                                              made.rearrange("p (s n) -> p s n", s=S)).then_inc(dirs_stored, 16)
                                act.wait_ge(emb_turned, it + 1)
                                for of, a, b in turns:
                                    last = nc.scalar.activation(turned[:, P * a:P * b], of[0:T * NB, 0:P * (b - a)], ACT.Copy)
                                last.then_inc(emb_ready, 1)
                                act.wait_ge(emb_ready, it + 1)
                                act.dma_start(emb_tab[ds(it * S, S)].rearrange("s k p -> k s p"),
                                              turned.rearrange("k (s p) -> k s p", s=S)).then_inc(emb_stored, 16)
                                act.wait_ge(dirs_stored, it * 16 + 16)
                                act.wait_ge(emb_stored, it * 16 + 16)

                        @block.vector
                        def _(dve):
                            move_windows(dve, moved, addressed)
                            with dve.Fori(0, ITERS) as it:
                                def add(q):
                                    dve.wait_ge(summed, it * S + (q + 1 + S))
                                    add_window(dve, it * S + q, 2, bank[q][:, 0:2 * W]).then_inc(window_added, 1)
                                    dve.wait_ge(window_added, it * S + (q + 1))

                                for q in range(S):
                                    dve.wait_ge(dst_in[q], it * 16 + 16)
                                    make_onehot(q, it * S + q).then_inc(onehot_made, 1)
                                    if q >= 1:
                                        add(q - 1)
                                    if q == 1:
                                        squared_norms(dve, it)
                                        squared_offsets(dve, it)
                                    if q == 3:
                                        directions(dve, it)
                                        embeddings(dve, it)
                                add(S - 1)
                    sig.clear()

        def second_pass():
            with ExitStack() as phase:
                sig = Signals(nc, phase)
                src_in, dst_in, rows_in, emb_in, weights_stored = (
                    sig.slots(n) for n in ("src_in", "dst_in", "rows_in", "emb_in", "weights_stored"))
                groups_begun = sig.one("groups_begun")
                moved, addressed, onehot_made, summed, window_added = sig.some(
                    "moved", "addressed", "onehot_made", "summed", "window_added")
                weights_seen, pre1, hidden1_made, pre2, hidden2_made, weights_multiplied, weights_made = sig.some(
                    "weights_seen", "pre1", "hidden1_made", "pre2", "hidden2_made", "weights_multiplied", "weights_made")
                hidden1, hidden2 = work[:, 0, 0:PAIRS * P], work[:, 1, 0:PAIRS * P]
                sums = [bank[q % 3][:, 0:W] for q in range(S)]
                psum_1, psum_2 = bank[3][:, 0:PAIRS * P], bank[4][:, 0:PAIRS * P]
                psum_w = [bank[5], bank[6]]

                start_rounds()
                with nc.Fori(0, span + 1, W):
                    with nc.Block() as block:
                        @block.sync
                        def _(sp):
                            def load(it, q):
                                sp.wait_ge(summed, it * S + (q + 1))
                                load_indices(sp, q, it * S + q, src_in, dst_in)
                                sp.dma_start(embT[:, q, :], group_of(emb_tab, it * S + q)).then_inc(emb_in[q], 16)

                            def store(it, q):
                                sp.wait_ge(weights_made, it * S + (q + 1))
                                sp.sem_inc(weights_seen, 1)
                                sp.dma_start(group_of(weight_tab, it * S + q), path_w[:, q, :]).then_inc(weights_stored[q], 16)

                            for q in range(S):
                                load(0, q)
                            with sp.Fori(1, ITERS) as it:
                                for q in range(S):
                                    load(it, q)
                                    store(it - 1, q)
                            for q in range(S):
                                store(ITERS - 1, q)
                            for q in range(S):
                                sp.wait_ge(weights_stored[q], 16 * ITERS)

                        @block.gpsimd
                        def _(pool):
                            gather_rows(pool, o_tab, src_in, rows_in, groups_begun)

                        @block.tensor
                        def _(pe):
                            pe.sem_inc(summed, S)

                            def add_tiles(q, tiles):
                                for t in tiles:
                                    last = nc.tensor.matmul(sums[q], gathered[:, q, D * t:D * (t + 1)], onehot[:, q, t, :],
                                                            start=(t == 0), stop=(t == T - 1))
                                return last

                            def step(it, q, first=False):
                                pe.wait_ge(emb_in[q], it * 16 + 16)
                                for j in range(PAIRS):
                                    last = nc.tensor.matmul(psum_1[:, P * j:P * (j + 1)], M0[:, j, :], embT[:, q, :], start=True, stop=True)
                                last.then_inc(pre1, 1)
                                pe.wait_ge(onehot_made, it * S + (q + 1))
                                if not (first and q < 2):
                                    pe.wait_ge(window_added, it * S + (q - 1))
                                pe.wait_ge(rows_in[q], it * 16 * T + 16 * T)
                                add_tiles(q, range(3))
                                pe.wait_ge(hidden1_made, it * S + (q + 1))
                                nc.tensor.matmul(psum_2, M1[:, :], hidden1, start=True, stop=True).then_inc(pre2, 1)
                                add_tiles(q, range(3, T)).then_inc(summed, 1)
                                if not (first and q == 0):
                                    pe.wait_ge(weights_made, it * S + q)
                                pe.wait_ge(hidden2_made, it * S + (q + 1))
                                for j in range(PAIRS):
                                    n = min(2, T - 2 * j) * D
                                    to = psum_w[j // 2][:, 2 * D * (j % 2):2 * D * (j % 2) + n]
                                    last = nc.tensor.matmul(to, hidden2[:, P * j:P * (j + 1)], M2[:, 0:n], start=True, stop=True)
                                last.then_inc(weights_multiplied, 1)

                            for q in range(S):
                                step(0, q, first=True)
                            with pe.Fori(1, ITERS) as it:
                                for q in range(S):
                                    step(it, q)

                        @block.scalar
                        def _(act):
                            with act.Fori(0, ITERS) as it:
                                for q in range(S):
                                    act.wait_ge(pre1, it * S + (q + 1))
                                    nc.scalar.activation(hidden1, psum_1, ACT.Silu, bias=MB0[:, :]).then_inc(hidden1_made, 1)
                                    act.wait_ge(pre2, it * S + (q + 1))
                                    nc.scalar.activation(hidden2, psum_2, ACT.Silu, bias=MB1[:, :]).then_inc(hidden2_made, 1)

                        @block.vector
                        def _(dve):
                            move_windows(dve, moved, addressed)

                            def make(it, q):
                                dve.wait_ge(dst_in[q], it * 16 + 16)
                                make_onehot(q, it * S + q).then_inc(onehot_made, 1)

                            def add(it, q):
                                dve.wait_ge(summed, it * S + (q + 1 + S))
                                add_window(dve, it * S + q, 1, sums[q]).then_inc(window_added, 1)
                                dve.wait_ge(window_added, it * S + (q + 1))

                            def keep_weights(it, q, reused):
                                dve.wait_ge(weights_multiplied, it * S + (q + 1))
                                if reused:
                                    dve.wait_ge(weights_stored[q], it * 16)
                                nc.vector.tensor_tensor(path_w[:, q, 0:4 * D].rearrange("p (t d) -> p t d", t=4),
                                                        psum_w[0][:, :].rearrange("p (t d) -> p t d", t=4),
                                                        spread(MB2[:, :].rearrange("p (a d) -> p a d", a=1), [P, 4, D]), ALU.add)
                                nc.vector.tensor_tensor(path_w[:, q, 4 * D:T * D], psum_w[1][:, 0:D], MB2[:, :], ALU.add).then_inc(weights_made, 1)

                            def steps(it, first=False, last=False):
                                for q in range(S):
                                    if q < S - 1:
                                        make(it, q + 1)
                                    elif not last:
                                        make(it + 1, 0)
                                    if q >= 1:
                                        add(it, q - 1)
                                    elif not first:
                                        add(it - 1, S - 1)
                                    keep_weights(it, q, not first)

                            make(0, 0)
                            steps(0, first=True)
                            if ITERS > 2:
                                with dve.Fori(1, ITERS - 1) as it:
                                    steps(it)
                            steps(ITERS - 1, last=True)
                            add(ITERS - 1, S - 1)
                    sig.clear()

        def message_pass():
            with ExitStack() as phase:
                sig = Signals(nc, phase)
                src_in, dst_in, rows_in, dirs_in, weights_in = (
                    sig.slots(n) for n in ("src_in", "dst_in", "rows_in", "dirs_in", "weights_in"))
                groups_begun = sig.one("groups_begun")
                moved, addressed, onehot_made, summed, window_added = sig.some(
                    "moved", "addressed", "onehot_made", "summed", "window_added")
                scalar_made, product_made, dot_step, dot_made, msgs_made = sig.some(
                    "scalar_made", "product_made", "dot_step", "dot_made", "msgs_made")
                sums = [bank[q][:, 0:2 * W] for q in range(S)]

                start_rounds()
                with nc.Fori(0, span + 1, W):
                    with nc.Block() as block:
                        @block.sync
                        def _(sp):
                            with sp.Fori(0, ITERS) as it:
                                for q in range(S):
                                    sp.wait_ge(summed, it * S + (q + 1))
                                    g = it * S + q
                                    load_indices(sp, q, g, src_in, dst_in)
                                    sp.dma_start(dirs[:, q, :], group_of(dir_tab, g)).then_inc(dirs_in[q], 16)
                                    sp.dma_start(path_w[:, q, :], group_of(weight_tab, g)).then_inc(weights_in[q], 16)

                        @block.gpsimd
                        def _(pool):
                            gather_rows(pool, up_tab, src_in, rows_in, groups_begun)

                        @block.tensor
                        def _(pe):
                            pe.sem_inc(summed, S)
                            with pe.Fori(0, ITERS) as it:
                                for q in range(S):
                                    pe.wait_ge(msgs_made, it * S + (q + 1))
                                    for half in range(2):
                                        for t in range(T):
                                            last = nc.tensor.matmul(sums[q][:, W * half:W * (half + 1)],
                                                                    msgs[:, q, 2 * D * t + D * half:2 * D * t + D * (half + 1)],
                                                                    onehot[:, q, t, :], start=(t == 0), stop=(t == T - 1))
                                    last.then_inc(summed, 1)

                        @block.vector
                        def _(dve):
                            dve.sem_inc(window_added, 1)
                            move_windows(dve, moved, addressed)

                            def add(it, q):
                                dve.wait_ge(summed, it * S + (q + 1 + S))
                                dve.wait_ge(window_added, it * S + (q + 1))
                                add_window(dve, it * S + q, 2, sums[q]).then_inc(window_added, 1)

                            def step(it, q):
                                n = it * S + (q + 1)
                                row = gathered[:, q, :].rearrange("p (t f) -> p t f", t=T)
                                s_row = row[:, :, 0:MUL]
                                v_row = row[:, :, MUL:D].rearrange("p t (c k) -> p t c k", c=3)
                                w = path_w[:, q, :].rearrange("p (t j k) -> p t j k", t=T, j=4)
                                m = msgs[:, q, :].rearrange("p (t j k) -> p t j k", t=T, j=8)
                                m3 = m[:, :, 1, :]
                                m1 = m[:, :, 2:8:2, :]
                                m2 = m[:, :, 3:8:2, :]
                                y = spread(dirs[:, q, :].rearrange("p (t c a) -> p t c a", t=T, a=1), [P, T, 3, MUL])

                                def thrice(ap):
                                    return spread(ap.rearrange("p t (a k) -> p t a k", a=1), [P, T, 3, MUL])

                                dve.wait_ge(dst_in[q], it * 16 + 16)
                                make_onehot(q, it * S + q).then_inc(onehot_made, 1)
                                dve.wait_ge(dirs_in[q], it * 16 + 16)
                                dve.wait_ge(rows_in[q], it * 16 * T + 16 * T)
                                nc.vector.tensor_tensor(m1, v_row, y, ALU.mult).then_inc(product_made, 1)
                                dve.wait_ge(weights_in[q], it * 16 + 16)
                                nc.vector.tensor_tensor(w[:, :, 1, :], w[:, :, 1, :], s_row, ALU.mult).then_inc(scalar_made, 1)
                                dve.wait_ge(product_made, n)
                                nc.vector.tensor_tensor(m3, m1[:, :, 0, :], m1[:, :, 1, :], ALU.add).then_inc(dot_step, 1)
                                nc.vector.tensor_tensor(m[:, :, 0, :], w[:, :, 0, :], s_row, ALU.mult)
                                dve.wait_ge(dot_step, n)
                                nc.vector.tensor_tensor(m3, m3, m1[:, :, 2, :], ALU.add).then_inc(dot_made, 1)
                                nc.vector.tensor_tensor(m2, thrice(w[:, :, 2, :]), v_row, ALU.mult)
                                dve.wait_ge(scalar_made, n)
                                dve.wait_ge(dot_made, n)
                                nc.vector.tensor_tensor(m1, thrice(w[:, :, 1, :]), y, ALU.mult)
                                nc.vector.scalar_tensor_tensor(out=m3, in0=m3, scalar=1.0 / math.sqrt(3.0), in1=w[:, :, 3, :],
                                                               op0=ALU.mult, op1=ALU.mult).then_inc(msgs_made, 1)

                            def steps(it, first=False):
                                for q in range(S):
                                    step(it, q)
                                    if q >= 2:
                                        add(it, q - 2)
                                    elif not first:
                                        add(it - 1, q + S - 2)

                            steps(0, first=True)
                            with dve.Fori(1, ITERS) as it:
                                steps(it)
                            for q in (S - 2, S - 1):
                                add(ITERS - 1, q)
                    sig.clear()

        def first_hop():
            with ExitStack() as phase:
                sig = Signals(nc, phase)
                h_in, o_stored = sig.slots("h_in"), sig.slots("o_stored")
                pool_waited = sig.one("pool_waited")
                waited, deg_kept, deg_inverted, mean_made, turned, turned_copied, o_free, product_made, biased, o_made = sig.some(
                    "waited", "deg_kept", "deg_inverted", "mean_made", "turned", "turned_copied", "o_free", "product_made", "biased", "o_made")
                with nc.Block() as block:
                    @block.sync
                    def _(sp):
                        sp.sem_inc(o_made, S)
                        with sp.Fori(0, CITERS) as it:
                            for q in range(S):
                                sp.wait_ge(o_made, it * S + (q + 1))
                                sp.dma_start(slot_a[q], chunk_of(h_tab, it * S + q)).then_inc(h_in[q], 16)

                    @block.vector
                    def _(dve):
                        with dve.Fori(0, CITERS) as it:
                            def mean(q):
                                s = it * S + (q + 1)
                                deg = agg[:, 1, ds((it * S + q) * CH, CH)]
                                nc.vector.tensor_scalar(deg, deg, 1.0, None, ALU.max).then_inc(deg_kept, 1)
                                dve.wait_ge(deg_kept, s)
                                dve.sem_inc(waited, 1)
                                nc.vector.reciprocal(deg, deg).then_inc(deg_inverted, 1)
                                dve.wait_ge(deg_inverted, s)
                                nc.vector.tensor_tensor(slot_sum[q], agg[:, 0, ds((it * S + q) * CH, CH)], deg, ALU.mult).then_inc(mean_made, 1)

                            def bias(q):
                                dve.wait_ge(product_made, it * S + (q + 1))
                                dve.wait_ge(o_free, it * S + (q + 1))
                                nc.vector.tensor_tensor(slot_b[q], rows_of(bank[2 + q]),
                                                        spread(B1[0:NR, :].rearrange("p (a d) -> p a d", a=1), [NR, NK, D]), ALU.add).then_inc(biased, 1)

                            for q in range(S):
                                mean(q)
                                if q >= 1:
                                    bias(q - 1)
                            bias(S - 1)

                    @block.tensor
                    def _(pe):
                        with pe.Fori(0, CITERS) as it:
                            for q in range(S):
                                s = it * S + (q + 1)
                                pe.wait_ge(h_in[q], it * 16 + 16)
                                pe.wait_ge(turned_copied, it * S + (q + 1))
                                to_features(q, slot_a[q]).then_inc(turned, 1)
                                pe.wait_ge(mean_made, s)
                                pe.wait_ge(turned_copied, it * S + (q + 3))
                                row_matmuls(bank[2 + q], [(strided(slot_sum[q]), W1L), (packed(slot_t[q]), W1R)]).then_inc(product_made, 1)

                    @block.scalar
                    def _(act):
                        act.sem_inc(turned_copied, 2)
                        act.sem_inc(o_free, S)
                        with act.Fori(0, CITERS) as it:
                            def finish(q):
                                act.wait_ge(biased, it * S + (q + 1))
                                nc.scalar.activation(slot_b[q], slot_b[q], ACT.Relu).then_inc(o_made, 1)

                            for q in range(S):
                                s = it * S + (q + 1)
                                act.wait_ge(turned, s)
                                nc.scalar.activation(slot_t[q], bank[q % 2][:, 0:CH], ACT.Copy).then_inc(turned_copied, 1)
                                act.wait_ge(mean_made, s)
                                nc.scalar.activation(agg[:, 0, ds((it * S + q) * CH, CH)], zeros[:, :], ACT.Copy)
                                if q >= 1:
                                    finish(q - 1)
                            finish(S - 1)
                        nc.scalar.activation(agg[:, 0, N:N + W], zeros[:, 0:W], ACT.Copy)

                    @block.gpsimd
                    def _(pool):
                        store_chunks(pool, o_tab, slot_b, o_made, o_stored, o_free, pool_waited)
                sig.clear()

        def second_hop():
            with ExitStack() as phase:
                sig = Signals(nc, phase)
                x_in, h_in, o_in, x2_stored, up_stored = (sig.slots(n) for n in ("x_in", "h_in", "o_in", "x2_stored", "up_stored"))
                mean_made, res_made, turned, turned_copied, product_made, res_biased, x2_made = sig.some(
                    "mean_made", "res_made", "turned", "turned_copied", "product_made", "res_biased", "x2_made")
                waited, pool_waited, stats_made, var_made, std_made, inverted, scales_made, h2_made = sig.some(
                    "waited", "pool_waited", "stats_made", "var_made", "std_made", "inverted", "scales_made", "h2_made")
                h2_turned, h2_copied, up_made, up_copied, slots_free = sig.some(
                    "h2_turned", "h2_copied", "up_made", "up_copied", "slots_free")
                with nc.Block() as block:
                    @block.sync
                    def _(sp):
                        sp.sem_inc(slots_free, S)
                        with sp.Fori(0, CITERS) as it:
                            for q in range(S):
                                c = it * S + q
                                sp.wait_ge(slots_free, it * S + (q + 1))
                                sp.dma_start(slot_b[q], chunk_of(x, c)).then_inc(x_in[q], 16)
                                sp.dma_start(slot_a[q], chunk_of(h_tab, c)).then_inc(h_in[q], 16)
                                sp.dma_start(slot_c[q], chunk_of(o_tab, c)).then_inc(o_in[q], 16)

                    @block.gpsimd
                    def _(pool):
                        bias = spread(B2[0:NR, :].rearrange("p (a d) -> p a d", a=1), [NR, NK, D])
                        with pool.Fori(0, CITERS) as it:
                            def store(q):
                                s = it * S + (q + 1)
                                pool.wait_ge(x2_made, s)
                                pool.sem_inc(pool_waited, 1)
                                pool.dma_start(chunk_of(x2_tab, it * S + q), slot_b[q]).then_inc(x2_stored[q], 16)
                                pool.wait_ge(up_copied, s)
                                pool.sem_inc(pool_waited, 1)
                                pool.dma_start(chunk_of(up_tab, it * S + q), slot_c[q]).then_inc(up_stored[q], 16)

                            def free(q):
                                pool.wait_ge(x2_stored[q], it * 16 + 16)
                                pool.wait_ge(up_stored[q], it * 16 + 16)
                                pool.sem_inc(slots_free, 1)

                            for q in range(S):
                                s = it * S + (q + 1)
                                pool.wait_ge(x_in[q], it * 16 + 16)
                                pool.wait_ge(h_in[q], it * 16 + 16)
                                pool.tensor_tensor(slot_b[q], slot_b[q], slot_a[q], ALU.add).then_inc(res_made, 1)
                                pool.wait_ge(res_made, s)
                                pool.tensor_tensor(slot_b[q], slot_b[q], bias, ALU.add).then_inc(res_biased, 1)
                                if q >= 1:
                                    store(q - 1)
                                if q >= 2:
                                    free(q - 2)
                            store(S - 1)
                            free(S - 2)
                            free(S - 1)
                        sig_reset(pool, x2_stored + up_stored)

                    @block.vector
                    def _(dve):
                        with dve.Fori(0, CITERS) as it:
                            def mean(q):
                                cols = ds((it * S + q) * CH, CH)
                                nc.vector.tensor_tensor(slot_sum[q], agg[:, 0, cols], agg[:, 1, cols], ALU.mult).then_inc(mean_made, 1)

                            def then(q):
                                s = it * S + (q + 1)
                                dve.wait_ge(product_made, s)
                                dve.wait_ge(res_biased, s)
                                nc.vector.tensor_tensor(slot_b[q], rows_of(bank[2 + q % 2]), slot_b[q], ALU.add).then_inc(x2_made, 1)
                                dve.wait_ge(x2_made, s)
                                row_stats(dve, q, slot_b[q], s, stats_made, var_made, std_made, inverted, scales_made, waited)

                            for q in range(S):
                                mean(q)
                                if q >= 1:
                                    then(q - 1)
                            then(S - 1)

                    @block.tensor
                    def _(pe):
                        with pe.Fori(0, CITERS) as it:
                            def first(q):
                                s = it * S + (q + 1)
                                pe.wait_ge(o_in[q], it * 16 + 16)
                                pe.wait_ge(turned_copied, s)
                                to_features(q, slot_c[q]).then_inc(turned, 1)
                                pe.wait_ge(mean_made, s)
                                pe.wait_ge(turned_copied, it * S + (q + 3))
                                row_matmuls(bank[2 + q % 2], [(strided(slot_sum[q]), W2L), (packed(slot_t[q]), W2R)]).then_inc(product_made, 1)

                            def then(q):
                                s = it * S + (q + 1)
                                pe.wait_ge(h2_made, s)
                                for k in range(NK):
                                    last = nc.tensor.transpose(bank[4][:, NR * k:NR * (k + 1)], slot_a[q][:, k, :], ident[0:NR, 0:NR])
                                last.then_inc(h2_turned, 1)
                                pe.wait_ge(h2_copied, s)
                                row_matmuls(bank[5], [(packed(slot_t[q]), WUP)]).then_inc(up_made, 1)

                            for q in range(S):
                                first(q)
                                if q >= 1:
                                    then(q - 1)
                            then(S - 1)

                    @block.scalar
                    def _(act):
                        act.sem_inc(turned_copied, 2)
                        with act.Fori(0, CITERS) as it:
                            def then(q):
                                s = it * S + (q + 1)
                                act.wait_ge(var_made, s)
                                row_std(q).then_inc(std_made, 1)
                                act.wait_ge(scales_made, s)
                                norm_relu(q, slot_a[q], slot_b[q]).then_inc(h2_made, 1)
                                act.wait_ge(h2_turned, s)
                                nc.scalar.activation(slot_t[q], bank[4][:, 0:CH], ACT.Copy).then_inc(h2_copied, 1)
                                act.wait_ge(up_made, s)
                                nc.scalar.activation(slot_c[q], rows_of(bank[5]), ACT.Copy, scale=1.0 / math.sqrt(MUL)).then_inc(up_copied, 1)

                            for q in range(S):
                                s = it * S + (q + 1)
                                act.wait_ge(turned, s)
                                nc.scalar.activation(slot_t[q], bank[q % 2][:, 0:CH], ACT.Copy).then_inc(turned_copied, 1)
                                act.wait_ge(mean_made, s)
                                for half in range(2):
                                    nc.scalar.activation(agg[:, half, ds((it * S + q) * CH, CH)], zeros[:, :], ACT.Copy)
                                if q >= 1:
                                    then(q - 1)
                            then(S - 1)
                        for half in range(2):
                            nc.scalar.activation(agg[:, half, N:N + W], zeros[:, 0:W], ACT.Copy)
                sig.clear()

        def output():
            with ExitStack() as phase:
                sig = Signals(nc, phase)
                x2_in, out_stored = sig.slots("x2_in"), sig.slots("out_stored")
                pool_waited = sig.one("pool_waited")
                sums_copied, product_made, out_made, out_free = sig.some("sums_copied", "product_made", "out_made", "out_free")
                with nc.Block() as block:
                    @block.sync
                    def _(sp):
                        sp.sem_inc(out_made, S)
                        with sp.Fori(0, CITERS) as it:
                            for q in range(S):
                                sp.wait_ge(out_made, it * S + (q + 1))
                                sp.dma_start(slot_a[q], chunk_of(x2_tab, it * S + q)).then_inc(x2_in[q], 16)

                    @block.scalar
                    def _(act):
                        with act.Fori(0, CITERS) as it:
                            for q in range(S):
                                cols = ds((it * S + q) * CH, CH)
                                act.wait_ge(out_made, it * S + (q + 1))
                                nc.scalar.activation(slot_sum[q], agg[:, 0, cols], ACT.Copy)
                                nc.scalar.activation(slot_t[q], agg[:, 1, cols], ACT.Copy).then_inc(sums_copied, 1)

                    @block.tensor
                    def _(pe):
                        with pe.Fori(0, CITERS) as it:
                            for q in range(S):
                                pe.wait_ge(sums_copied, it * S + (q + 1))
                                row_matmuls(bank[q], [(strided(slot_sum[q]), WOA), (strided(slot_t[q]), WOB)]).then_inc(product_made, 1)

                    @block.vector
                    def _(dve):
                        dve.sem_inc(out_free, S)
                        with dve.Fori(0, CITERS) as it:
                            for q in range(S):
                                dve.wait_ge(x2_in[q], it * 16 + 16)
                                dve.wait_ge(out_free, it * S + (q + 1))
                                dve.wait_ge(product_made, it * S + (q + 1))
                                nc.vector.scalar_tensor_tensor(
                                    out=slot_b[q].rearrange("p k d -> p (k d)"), in0=bank[q][0:NR, :],
                                    scalar=1.0 / (math.sqrt(2 * MUL) * AVG), in1=slot_a[q].rearrange("p k d -> p (k d)"),
                                    op0=ALU.mult, op1=ALU.add).then_inc(out_made, 1)

                    @block.gpsimd
                    def _(pool):
                        store_chunks(pool, out, slot_b, out_made, out_stored, out_free, pool_waited)
                sig.clear()

        first_pass()
        first_hop()
        second_pass()
        second_hop()
        message_pass()
        output()


INPUTS = ["x", "src", "dst", "edge_attr_3", "edge_weight",
          "L0_gnn_W1_l", "L0_gnn_W1_r", "L0_gnn_b1", "L0_gnn_W2_l", "L0_gnn_W2_r", "L0_gnn_b2",
          "L1_gnn_W_up0", "L1_gnn_W_up1", "L1_gnn_mlp_w0", "L1_gnn_mlp_b0", "L1_gnn_mlp_w1", "L1_gnn_mlp_b1",
          "L1_gnn_mlp_w2", "L1_gnn_mlp_b2", "L1_gnn_W_out0", "L1_gnn_W_out1"]


def kernel(**inputs):
    import numpy as np
    from concourse import bacc
    from concourse.bass_utils import run_bass_kernel_spmd

    nc = bacc.Bacc("TRN2", target_bir_lowering=False, num_devices=1)
    arrays, args = {}, []
    for name in INPUTS:
        a = np.ascontiguousarray(inputs[name])
        arrays[f"in_{name}"] = a
        args.append(nc.dram_tensor(f"in_{name}", a.shape, mybir.dt.from_np(a.dtype), kind="ExternalInput").ap())
    out = nc.dram_tensor("out", inputs["x"].shape, F32, kind="ExternalOutput").ap()
    program(nc, *args, out)
    r = run_bass_kernel_spmd(nc, [arrays], core_ids=[0])
    return r.results[0]["out"]
```

```python
import math
from contextlib import ExitStack

import concourse.bass as bass
from concourse import mybir

F32 = mybir.dt.float32
I32 = mybir.dt.int32
ALU = mybir.AluOpType
ACT = mybir.ActivationFunctionType
AX = mybir.AxisListType
ds = bass.ds

P = 128
T = 5
S = 5
W = 64
GE = P * T
ST = S * T
NR, NK = 125, 4
CH = NR * NK
D = 128
MUL = 32
NB = 8
HID = 64
PAIRS = (T + 1) // 2
LN_EPS = 1e-5
AVG = 16.0


class Signals:

    def __init__(self, nc, ctx):
        self.nc, self.ctx, self.made = nc, ctx, []

    def one(self, name):
        s = self.ctx.enter_context(self.nc.semaphore(name))
        self.made.append(s)
        return s

    def some(self, *names):
        return [self.one(n) for n in names]

    def slots(self, name):
        return [self.one(f"{name}{q}") for q in range(S)]

    def clear(self):
        for r in runs(self.made):
            self.nc.all_engine_barrier(sems_to_clear=r)


def runs(semaphores):
    numbers = sorted(s.num for s in semaphores)
    starts = [n for n in numbers if n - 1 not in numbers]
    ends = [n + 1 for n in numbers if n + 1 not in numbers]
    return [range(a, b) for a, b in zip(starts, ends)]


def sig_reset(pool, semaphores):
    for r in runs(semaphores):
        pool.dma_reset(r)




def spread(ap, shape):
    return ap.broadcast_to(list(shape))


def program(nc, x, src, dst, attr, weight, w1l, w1r, b1, w2l, w2r, b2, up0, up1,
            m0, mb0, m1, mb1, m2, mb2, wo0, wo1, out):
    N = x.shape[0]
    E = src.shape[0]
    GROUPS = E // GE
    ITERS = GROUPS // S
    CHUNKS = N // CH
    CITERS = CHUNKS // S
    GP = GROUPS // S
    RN = N // ITERS
    assert GROUPS * GE == E and ITERS * S == GROUPS and CHUNKS * CH == N and CITERS * S == CHUNKS
    assert GP <= P and RN * ITERS == N and RN <= P

    def table(name, shape, dt=F32):
        return nc.dram_tensor(name, shape, dt, kind="Internal").ap()

    h_tab, o_tab, x2_tab, up_tab = (table(n, [N, D]) for n in ("h_tab", "o_tab", "x2_tab", "up_tab"))
    root1_tab, root2_tab = table("root1_tab", [N, D]), table("root2_tab", [N, D])
    base_tab = table("base_tab", [1, GROUPS], I32)
    dir_tab = table("dir_tab", [GROUPS, P, T * 3])
    emb_tab = table("emb_tab", [GROUPS, T * NB, P])
    weight_tab = table("weight_tab", [GROUPS, P, T * D])

    src_v = src.rearrange("(g p t) -> g p t", p=P, t=T)
    dst_v = dst.rearrange("(g p t) -> g p t", p=P, t=T)
    attr_v = attr.rearrange("(g p t) c -> g p (t c)", p=P, t=T)
    weight_v = weight.rearrange("(g p t) -> g p t", p=P, t=T)

    def group_of(view, g):
        return view[ds(g, 1)].rearrange("g p n -> (g p) n")

    def chunk_of(tab, c):
        return tab.rearrange("(c p k) d -> c p k d", p=NR, k=NK)[ds(c, 1)].rearrange("c p k d -> (c p) k d")

    def root_rows(tab, i):
        return tab.rearrange("(i p) d -> i p d", p=RN)[ds(i, 1)].rearrange("i p d -> (i p) d")

    with ExitStack() as ctx:
        def sb(name, shape, dt=F32):
            return ctx.enter_context(nc.sbuf_tensor(name, shape, dt))

        agg = sb("agg", [P, 2, N + W])
        gathered = sb("gathered", [P, S, T * D])
        msgs = sb("msgs", [P, S, T * 2 * D])
        path_w = sb("path_w", [P, S, T * D])
        onehot = sb("onehot", [P, S, T, W])
        src_i = sb("src_i", [P, S, T], I32)
        dst_i = sb("dst_i", [P, S, T], I32)
        dirs = sb("dirs", [P, S, T * 3])
        embT = sb("embT", [T * NB, S, P])
        work = sb("work", [P, S, 512])
        slot_a = [gathered[0:NR, q, 0:512].rearrange("p (k d) -> p k d", k=NK) for q in range(S)]
        slot_b = [msgs[0:NR, q, 0:512].rearrange("p (k d) -> p k d", k=NK) for q in range(S)]
        slot_c = [msgs[0:NR, q, 512:1024].rearrange("p (k d) -> p k d", k=NK) for q in range(S)]
        slot_sum = [path_w[:, q, 0:CH] for q in range(S)]
        slot_t = [work[:, q, 0:CH] for q in range(S)]
        slot_deg = [work[0:1, q, 0:CH] for q in range(S)]
        root_x, root_h, root_o, root_t, root_sum = (msgs[:, 2, D * i:D * (i + 1)] for i in range(5))
        inv_deg = sb("inv_deg", [NR, CHUNKS * NK])
        group_base = sb("group_base", [P, GROUPS])
        round_base = sb("round_base", [P, GROUPS])
        addr_i = sb("addr_i", [P, GROUPS], I32)
        span_i = sb("span_i", [1, 1], I32)
        extremes = sb("extremes", [P, 12])
        iota_w = sb("iota_w", [P, W])
        centres = sb("centres", [P, NB])
        ident, ones = sb("ident", [P, P]), sb("ones", [P, P])
        zeros = sb("zeros", [P, CH])
        eps = sb("eps", [P, 1])
        bn6, mean_var = sb("bn6", [P, S, NK, 6]), sb("mean_var", [P, S, NK, 2])
        rstd, shift = sb("rstd", [P, S, NK]), sb("shift", [P, S, NK])
        W1L, W1R, W2L, W2R, WUP, WOA, WOB = (sb(n, [D, D]) for n in ("W1L", "W1R", "W2L", "W2R", "WUP", "WOA", "WOB"))
        B1, B2 = sb("B1", [P, D]), sb("B2", [P, D])
        M0 = sb("M0", [T * NB, PAIRS, P])
        M1 = sb("M1", [P, P])
        M2 = sb("M2", [P, 2 * D])
        MB0, MB1 = sb("MB0", [P, 1]), sb("MB1", [P, 1])
        MB2 = sb("MB2", [P, D])
        stage = sb("stage", [P, 2, MUL])
        bank = [ctx.enter_context(nc.psum_tensor(f"bank{i}", [P, 512], F32)) for i in range(8)]

        with ExitStack() as phase:
            sig = Signals(nc, phase)
            dst_loaded, loaded, placed, staged, base_out, base_in = sig.some(
                "dst_loaded", "loaded", "placed", "staged", "base_out", "base_in")
            filled, ident_made, extremes_made, least_made, span_step, span_t, base_made = sig.some(
                "filled", "ident_made", "extremes_made", "least_made", "span_step", "span_t", "base_made")
            dst_rows = gathered[0:GP, :, :].rearrange("p s n -> p (s n)").bitcast(I32)
            least, most = extremes[0:GP, 0:S], extremes[0:GP, S:2 * S]
            least_i = src_i[0:GP, 0, :]
            OUT1 = [(WOA, 64, 0, 0), (WOB, 0, 1, 1), (WOB, 64, 1, 2)]

            with nc.Block() as block:
                @block.sync
                def _(sp):
                    sp.dma_start(dst_rows, dst.rearrange("(p n) -> p n", p=GP)).then_inc(dst_loaded, 16)
                    n = 0
                    for to, of in ((W1L, w1l), (W1R, w1r), (W2L, w2l), (W2R, w2r)):
                        sp.dma_start(to[:, :], of).then_inc(loaded, 16)
                        n += 1
                    for to, of in ((B1, b1), (B2, b2), (MB2, mb2)):
                        sp.dma_start(to[:, :], spread(of.rearrange("(a n) -> a n", a=1), [P, D])).then_inc(loaded, 16)
                        n += 1
                    for j in range(2):
                        for to, of in ((MB0, mb0), (MB1, mb1)):
                            sp.dma_start(to[HID * j:HID * (j + 1), :], of.rearrange("(n a) -> n a", a=1)).then_inc(loaded, 16)
                            n += 1
                    for _, row, a, _ in OUT1:
                        sp.dma_start(stage[row:row + 2 * MUL, a, :], wo1).then_inc(staged, 16)
                    sp.wait_ge(filled, 1)
                    blocks = [(WUP[0:MUL, 0:MUL], up0), (WOA[0:2 * MUL, 0:MUL], wo0)]
                    blocks += [(WUP[MUL + c:MUL + c + 3 * (MUL - 1) + 1:3, MUL * (1 + c):MUL * (2 + c)], up1) for c in range(3)]
                    blocks += [(M0[NB * t:NB * (t + 1), t // 2, HID * (t % 2):HID * (t % 2 + 1)], m0) for t in range(T)]
                    blocks += [(M1[HID * j:HID * (j + 1), HID * j:HID * (j + 1)], m1) for j in range(2)]
                    blocks += [(M2[HID * j:HID * (j + 1), D * j:D * (j + 1)], m2) for j in range(2)]
                    for to, of in blocks:
                        sp.dma_start(to, of).then_inc(placed, 16)
                    sp.wait_ge(least_made, 1)
                    sp.dma_start(base_tab.rearrange("a (p s) -> (a p) s", s=S), least_i).then_inc(base_out, 16)
                    sp.wait_ge(base_out, 16)
                    sp.dma_start(addr_i[:, :], spread(base_tab, [P, GROUPS])).then_inc(base_in, 16)
                    sp.wait_ge(loaded, 16 * n)
                    sp.wait_ge(placed, 16 * len(blocks))

                @block.gpsimd
                def _(pool):
                    for tile in (WUP, WOA, WOB, M1, M2, zeros, ident):
                        pool.memset(tile[:, :], 0.0)
                    pool.memset(M0[:, :, :], 0.0)
                    pool.memset(eps[:, :], LN_EPS)
                    pool.memset(ones[:, :], 1.0).then_inc(filled, 1)
                    pool.wait_ge(filled, 1)
                    pool.affine_select(out=ident[:, :], in_=ident[:, :], compare_op=ALU.not_equal, fill=1.0,
                                       base=0, pattern=[[-1, P]], channel_multiplier=1)
                    pool.iota(iota_w[:, :], [[1, W]], base=0, channel_multiplier=0,
                              allow_small_or_imprecise_dtypes=True).then_inc(ident_made, 1)
                    pool.memset(agg[:, 1, :], 0.0)

                @block.vector
                def _(dve):
                    dve.wait_ge(dst_loaded, 16)
                    rows = dst_rows.rearrange("p (s e) -> p s e", s=S)
                    nc.vector.tensor_reduce(least, rows, axis=AX.X, op=ALU.min).then_inc(extremes_made, 1)
                    nc.vector.tensor_reduce(most, rows, axis=AX.X, op=ALU.max).then_inc(extremes_made, 1)
                    dve.wait_ge(extremes_made, 2)
                    nc.vector.tensor_copy(least_i, least).then_inc(least_made, 1)
                    nc.vector.tensor_tensor(most, most, least, ALU.subtract).then_inc(span_step, 1)
                    dve.wait_ge(span_step, 1)
                    nc.vector.tensor_reduce(extremes[0:GP, 10:11], most, axis=AX.X, op=ALU.max).then_inc(span_step, 1)
                    dve.wait_ge(span_t, 1)
                    nc.vector.tensor_reduce(extremes[0:1, 11:12], bank[0][0:1, 0:GP], axis=AX.X, op=ALU.max).then_inc(span_step, 1)
                    dve.wait_ge(span_step, 3)
                    nc.vector.tensor_copy(span_i[:, :], extremes[0:1, 11:12])
                    dve.wait_ge(ident_made, 1)
                    nc.vector.tensor_scalar(centres[:, :], iota_w[:, 0:NB], 1.0 / (NB - 1), None, ALU.mult)
                    nc.vector.memset(agg[:, 0, :], 0.0)
                    dve.wait_ge(staged, 48)
                    for to, row, a, c in OUT1:
                        nc.vector.tensor_copy(to[row:row + 2 * MUL, MUL + c:MUL + c + 3 * (MUL - 1) + 1:3], stage[row:row + 2 * MUL, a, :])
                    dve.wait_ge(base_in, 16)
                    nc.vector.tensor_copy(group_base[:, :], addr_i[:, :])

                @block.tensor
                def _(pe):
                    pe.wait_ge(ident_made, 1)
                    pe.wait_ge(span_step, 2)
                    nc.tensor.transpose(bank[0][0:1, 0:GP], extremes[0:GP, 10:11], ident[0:GP, 0:GP]).then_inc(span_t, 1)
            sig.clear()

        span = nc.values_load(span_i[0:1, 0:1], min_val=0, max_val=N - 1)

        def chunk_steps(engine, *stages):
            def step(it, q, first=False):
                for lag, make in stages:
                    if q >= lag:
                        make(it, q - lag)
                    elif not first:
                        make(it - 1, q - lag + S)

            for q in range(S):
                step(0, q, first=True)
            if CITERS > 1:
                with engine.Fori(1, CITERS) as it:
                    for q in range(S):
                        step(it, q)
            for late in range(1, max(lag for lag, _ in stages) + 1):
                for lag, make in stages:
                    if late <= lag:
                        make(CITERS - 1, S - 1 + late - lag)

        def row_stats(dve, q, rows, s, stats_made, var_made, waited):
            for k in range(NK):
                last = nc.vector.bn_stats(bn6[0:NR, q, k, :], rows[:, k, :])
            last.then_inc(stats_made, 1)
            dve.wait_ge(stats_made, s)
            dve.sem_inc(waited, 1)
            for k in range(NK):
                last = nc.vector.bn_aggr(mean_var[0:NR, q, k, :], bn6[0:NR, q, k, :])
            last.then_inc(var_made, 1)

        def invert_std(dve, q, s, std_made, inverted):
            dve.wait_ge(std_made, s)
            nc.vector.reciprocal(rstd[0:NR, q, :], rstd[0:NR, q, :]).then_inc(inverted, 1)
            dve.wait_ge(inverted, s)

        def row_std(q):
            return nc.scalar.activation(rstd[0:NR, q, :], mean_var[0:NR, q, :, 1], ACT.Sqrt, bias=eps[0:NR, :])

        def norm_relu(q, to, rows):
            for k in range(NK):
                last = nc.scalar.activation(to[:, k, :], rows[:, k, :], ACT.Relu,
                                            bias=shift[0:NR, q, k:k + 1], scale=rstd[0:NR, q, k:k + 1])
            return last

        def row_matmuls(to, terms):
            for k in range(NK):
                for i, (cols, weights) in enumerate(terms):
                    last = nc.tensor.matmul(to[0:NR, D * k:D * (k + 1)], cols(k), weights[:, :],
                                            start=(i == 0), stop=(i == len(terms) - 1))
            return last

        def strided(tile):
            return lambda k: tile[:, k:k + NK * (NR - 1) + 1:NK]

        def packed(tile):
            return lambda k: tile[:, NR * k:NR * (k + 1)]

        def rows_of(psum):
            return psum[0:NR, :].rearrange("p (k d) -> p k d", k=NK)

        def store_chunks(pool, tab, slots, made, stored, free, waited):
            with pool.Fori(0, CITERS) as it:
                for q in range(S):
                    pool.wait_ge(made, it * S + (q + 1 + S))
                    pool.sem_inc(waited, 1)
                    pool.dma_start(chunk_of(tab, it * S + q), slots[q]).then_inc(stored[q], 16)
                    if q >= 1:
                        pool.wait_ge(stored[q - 1], it * 16 + 16)
                        pool.sem_inc(free, 1)
                pool.wait_ge(stored[S - 1], it * 16 + 16)
                pool.sem_inc(free, 1)
            sig_reset(pool, stored)

        def scaled_plus(to, psum, c, rows):
            for k in range(NK):
                last = nc.vector.scalar_tensor_tensor(out=to[:, k, :], in0=psum[0:NR, D * k:D * (k + 1)],
                                                      scalar=inv_deg[:, ds(c * NK + k, 1)], in1=rows[:, k, :],
                                                      op0=ALU.mult, op1=ALU.add)
            return last

        with ExitStack() as phase:
            sig = Signals(nc, phase)
            x_in, h_stored = sig.slots("x_in"), sig.slots("h_stored")
            waited, stats_made, var_made, std_made, inverted, scales_made, h_made = sig.some(
                "waited", "stats_made", "var_made", "std_made", "inverted", "scales_made", "h_made")
            h_free, pool_waited = sig.some("h_free", "pool_waited")
            with nc.Block() as block:
                @block.sync
                def _(sp):
                    sp.sem_inc(h_made, S)
                    with sp.Fori(0, CITERS) as it:
                        for q in range(S):
                            sp.wait_ge(h_made, it * S + (q + 1))
                            sp.dma_start(slot_a[q], chunk_of(x, it * S + q)).then_inc(x_in[q], 16)

                @block.vector
                def _(dve):
                    def stats(it, q):
                        dve.wait_ge(x_in[q], it * 16 + 16)
                        row_stats(dve, q, slot_a[q], it * S + (q + 1), stats_made, var_made, waited)

                    def scales(it, q):
                        invert_std(dve, q, it * S + (q + 1), std_made, inverted)
                        nc.vector.scalar_tensor_tensor(out=shift[0:NR, q, :], in0=mean_var[0:NR, q, :, 0], scalar=-1.0,
                                                       in1=rstd[0:NR, q, :], op0=ALU.mult, op1=ALU.mult).then_inc(scales_made, 1)

                    chunk_steps(dve, (0, stats), (1, scales))

                @block.scalar
                def _(act):
                    def std(it, q):
                        act.wait_ge(var_made, it * S + (q + 1))
                        row_std(q).then_inc(std_made, 1)

                    def norm(it, q):
                        act.wait_ge(scales_made, it * S + (q + 1))
                        act.wait_ge(h_free, it * S + (q + 1))
                        norm_relu(q, slot_b[q], slot_a[q]).then_inc(h_made, 1)

                    act.sem_inc(h_free, S)
                    chunk_steps(act, (0, std), (1, norm))

                @block.gpsimd
                def _(pool):
                    store_chunks(pool, h_tab, slot_b, h_made, h_stored, h_free, pool_waited)
            sig.clear()

        def start_rounds():
            with nc.Block() as block:
                @block.vector
                def _(dve):
                    nc.vector.tensor_scalar(round_base[:, :], group_base[:, :], float(-W), None, ALU.add)

        def move_windows(dve, moved, addressed):
            nc.vector.tensor_scalar(round_base[:, :], round_base[:, :], float(W), None, ALU.add).then_inc(moved, 1)
            dve.wait_ge(moved, 1)
            nc.vector.tensor_scalar(addr_i[0:1, :], round_base[0:1, :], float(N), None, ALU.min).then_inc(addressed, 1)
            dve.wait_ge(addressed, 1)

        def load_indices(sp, q, g, src_in, dst_in):
            sp.dma_start(src_i[:, q, :], group_of(src_v, g)).then_inc(src_in[q], 16)
            sp.dma_start(dst_i[:, q, :], group_of(dst_v, g)).then_inc(dst_in[q], 16)

        def gather_rows(pool, rows_of_table, src_in, rows_in, groups_begun):
            with pool.Fori(0, ITERS) as it:
                for q in range(S):
                    pool.wait_ge(src_in[q], it * 16 + 16)
                    pool.sem_inc(groups_begun, 1)
                    for t in range(T):
                        pool.indirect_dma_start(
                            out=gathered[:, q, D * t:D * (t + 1)], out_offset=None, in_=rows_of_table,
                            in_offset=bass.IndirectOffsetOnAxis(ap=src_i[:, q, t:t + 1], axis=0)).then_inc(rows_in[q], 16)
            for q in range(S):
                pool.wait_ge(rows_in[q], 16 * T * ITERS)
            sig_reset(pool, rows_in)

        def make_onehot(q, g):
            return nc.vector.scalar_tensor_tensor(
                out=onehot[:, q, :, :], in0=spread(dst_i[:, q, :].rearrange("p (t a) -> p t a", a=1), [P, T, W]),
                scalar=round_base[:, ds(g, 1)], in1=spread(iota_w[:, :].rearrange("p (a j) -> p a j", a=1), [P, T, W]),
                op0=ALU.subtract, op1=ALU.is_equal)

        def add_window(dve, g, halves, sums):
            at = dve.value_load(addr_i[0:1, ds(g, 1)], min_val=0, max_val=N)
            where = agg[:, 0:halves, ds(at, W)]
            return nc.vector.tensor_tensor(where, where, sums.rearrange("p (a j) -> p a j", a=halves), ALU.add)

        def along(ap, n):
            return spread(ap.rearrange("p (e a) -> p e a", a=1), [P, ap.shape[1], n])

        root_turn, root_psum = bank[7][:, 0:RN], bank[7][:, 2 * D:3 * D]

        def turn_root_rows(pe, it, rows, root_in, landed, root_made, root_turned):
            pe.wait_ge(root_in, it * landed + landed)
            pe.wait_ge(root_made, it + 1)
            nc.tensor.transpose(root_turn, rows[0:RN, :], ident[0:RN, 0:RN]).then_inc(root_turned, 1)

        def copy_root_columns(act, it, root_turned, root_copied):
            act.wait_ge(root_turned, it + 2)
            nc.scalar.activation(root_t[:, 0:RN], root_turn, ACT.Copy).then_inc(root_copied, 1)

        def root_product(pe, it, weights, root_copied, root_multiplied):
            pe.wait_ge(root_copied, it + 1)
            nc.tensor.matmul(root_psum[0:RN, :], root_t[:, 0:RN], weights[:, :], start=True, stop=True).then_inc(root_multiplied, 1)

        def first_pass():
            with ExitStack() as phase:
                sig = Signals(nc, phase)
                src_in, dst_in, rows_in = sig.slots("src_in"), sig.slots("dst_in"), sig.slots("rows_in")
                groups_begun = sig.one("groups_begun")
                moved, addressed, onehot_made, summed, window_added = sig.some(
                    "moved", "addressed", "onehot_made", "summed", "window_added")
                vec_in, squared, norm2_made, norm_made, norm_kept, norm_inverted, dirs_made, dirs_stored = sig.some(
                    "vec_in", "squared", "norm2_made", "norm_made", "norm_kept", "norm_inverted", "dirs_made", "dirs_stored")
                len_in, clipped, offset_made, square_made, gauss_made, emb_made, emb_turned, emb_ready, emb_stored = sig.some(
                    "len_in", "clipped", "offset_made", "square_made", "gauss_made", "emb_made", "emb_turned", "emb_ready", "emb_stored")
                root_in, root_turned, root_copied, root_multiplied, root_made, root_stored = sig.some(
                    "root_in", "root_turned", "root_copied", "root_multiplied", "root_made", "root_stored")
                vec, sq, made = (work[:, i, 0:ST * 3] for i in range(3))
                norm2, norm, kept, inverse, length, clip, inside = (work[:, 3, 32 * i:32 * i + ST] for i in range(7))
                offset, square, gauss, emb = (msgs[:, 1, 256 * i:256 * i + ST * NB] for i in range(4))
                turned = msgs[0:T * NB, 0, 0:S * P]
                turns = [(bank[5], 0, 4), (bank[6], 4, S)]

                def by_edge(ap, n):
                    return ap.rearrange("p (e c) -> p e c", c=n)

                def squared_norms(dve, it):
                    dve.wait_ge(vec_in, it * 16 + 16)
                    nc.vector.tensor_tensor(sq, vec, vec, ALU.mult).then_inc(squared, 1)
                    dve.wait_ge(squared, it + 1)
                    nc.vector.tensor_reduce(norm2, by_edge(sq, 3), axis=AX.X, op=ALU.add).then_inc(norm2_made, 1)

                def squared_offsets(dve, it):
                    dve.wait_ge(len_in, it * 16 + 16)
                    nc.vector.tensor_scalar(clip, length, 0.0, 1.0, ALU.max, ALU.min)
                    nc.vector.tensor_scalar(inside, length, 1.0, math.sqrt(NB), ALU.is_le, ALU.mult).then_inc(clipped, 1)
                    dve.wait_ge(clipped, it + 1)
                    nc.vector.tensor_tensor(by_edge(offset, NB), along(clip, NB),
                                            spread(centres[:, :].rearrange("p (a k) -> p a k", a=1), [P, ST, NB]),
                                            ALU.subtract).then_inc(offset_made, 1)
                    dve.wait_ge(offset_made, it + 1)
                    nc.vector.tensor_tensor(square, offset, offset, ALU.mult).then_inc(square_made, 1)

                def directions(dve, it):
                    dve.wait_ge(norm_made, it + 1)
                    nc.vector.tensor_scalar(kept, norm, 1e-12, None, ALU.add).then_inc(norm_kept, 1)
                    dve.wait_ge(norm_kept, it + 1)
                    nc.vector.reciprocal(inverse, kept).then_inc(norm_inverted, 1)
                    dve.wait_ge(norm_inverted, it + 1)
                    nc.vector.scalar_tensor_tensor(out=by_edge(made, 3), in0=by_edge(vec, 3), scalar=math.sqrt(3.0),
                                                   in1=along(inverse, 3), op0=ALU.mult, op1=ALU.mult).then_inc(dirs_made, 1)

                def embeddings(dve, it):
                    dve.wait_ge(gauss_made, it + 1)
                    nc.vector.tensor_tensor(by_edge(emb, NB), by_edge(gauss, NB), along(inside, NB), ALU.mult).then_inc(emb_made, 1)

                start_rounds()
                with nc.Fori(0, span + 1, W):
                    with nc.Block() as block:
                        @block.sync
                        def _(sp):
                            sp.sem_inc(dirs_made, 1)
                            sp.sem_inc(emb_made, 1)
                            sp.sem_inc(root_turned, 1)
                            sp.sem_inc(root_made, 1)
                            with sp.Fori(0, ITERS) as it:
                                for q in range(S):
                                    sp.wait_ge(summed, it * S + (q + 1))
                                    load_indices(sp, q, it * S + q, src_in, dst_in)
                                    if q == 0:
                                        sp.wait_ge(dirs_made, it + 1)
                                        sp.dma_start(vec.rearrange("p (s n) -> p s n", s=S),
                                                     attr_v[ds(it * S, S)].rearrange("s p n -> p s n")).then_inc(vec_in, 16)
                                        sp.wait_ge(emb_made, it + 1)
                                        sp.dma_start(length.rearrange("p (s n) -> p s n", s=S),
                                                     weight_v[ds(it * S, S)].rearrange("s p n -> p s n")).then_inc(len_in, 16)
                                        sp.wait_ge(root_turned, it + 1)
                                        sp.dma_start(root_h[0:RN, :], root_rows(h_tab, it)).then_inc(root_in, 16)

                        @block.gpsimd
                        def _(pool):
                            gather_rows(pool, h_tab, src_in, rows_in, groups_begun)

                        @block.tensor
                        def _(pe):
                            pe.sem_inc(summed, S)
                            with pe.Fori(0, ITERS) as it:
                                for q in range(S):
                                    pe.wait_ge(onehot_made, it * S + (q + 1))
                                    for t in range(T):
                                        nc.tensor.matmul(bank[q][:, W:2 * W], ones[:, :], onehot[:, q, t, :], start=(t == 0), stop=(t == T - 1))
                                    if q == S - 1:
                                        pe.wait_ge(emb_made, it + 2)
                                    pe.wait_ge(rows_in[q], it * 16 * T + 16 * T)
                                    for t in range(T):
                                        last = nc.tensor.matmul(bank[q][:, 0:W], gathered[:, q, D * t:D * (t + 1)], onehot[:, q, t, :],
                                                                start=(t == 0), stop=(t == T - 1))
                                    last.then_inc(summed, 1)
                                    if q == 0:
                                        turn_root_rows(pe, it, root_h, root_in, 16, root_made, root_turned)
                                    if q == 2:
                                        root_product(pe, it, W1R, root_copied, root_multiplied)
                                for to, a, b in turns:
                                    for j in range(a, b):
                                        last = nc.tensor.transpose(to[0:T * NB, P * (j - a):P * (j - a + 1)],
                                                                   emb[:, T * NB * j:T * NB * (j + 1)], ident[:, :])
                                last.then_inc(emb_turned, 1)

                        @block.scalar
                        def _(act):
                            with act.Fori(0, ITERS) as it:
                                act.wait_ge(norm2_made, it + 1)
                                nc.scalar.activation(norm, norm2, ACT.Sqrt).then_inc(norm_made, 1)
                                act.wait_ge(square_made, it + 1)
                                nc.scalar.activation(gauss, square, ACT.Exp, scale=-0.5 * (NB - 1) ** 2).then_inc(gauss_made, 1)
                                copy_root_columns(act, it, root_turned, root_copied)
                                act.wait_ge(dirs_made, it + 2)
                                act.dma_start(dir_tab[ds(it * S, S)].rearrange("s p n -> p s n"),
                                              made.rearrange("p (s n) -> p s n", s=S)).then_inc(dirs_stored, 16)
                                act.wait_ge(emb_turned, it + 1)
                                for of, a, b in turns:
                                    last = nc.scalar.activation(turned[:, P * a:P * b], of[0:T * NB, 0:P * (b - a)], ACT.Copy)
                                last.then_inc(emb_ready, 1)
                                act.wait_ge(emb_ready, it + 1)
                                act.dma_start(emb_tab[ds(it * S, S)].rearrange("s k p -> k s p"),
                                              turned.rearrange("k (s p) -> k s p", s=S)).then_inc(emb_stored, 16)
                                act.wait_ge(root_made, it + 2)
                                act.dma_start(root_rows(root1_tab, it), root_sum[0:RN, :]).then_inc(root_stored, 16)
                                act.wait_ge(root_stored, it * 16 + 16)
                                act.wait_ge(dirs_stored, it * 16 + 16)
                                act.wait_ge(emb_stored, it * 16 + 16)

                        @block.vector
                        def _(dve):
                            move_windows(dve, moved, addressed)
                            with dve.Fori(0, ITERS) as it:
                                def add(q):
                                    dve.wait_ge(summed, it * S + (q + 1 + S))
                                    add_window(dve, it * S + q, 2, bank[q][:, 0:2 * W]).then_inc(window_added, 1)
                                    dve.wait_ge(window_added, it * S + (q + 1))

                                for q in range(S):
                                    dve.wait_ge(dst_in[q], it * 16 + 16)
                                    make_onehot(q, it * S + q).then_inc(onehot_made, 1)
                                    if q >= 1:
                                        add(q - 1)
                                    if q == 1:
                                        squared_norms(dve, it)
                                        squared_offsets(dve, it)
                                    if q == 3:
                                        directions(dve, it)
                                        embeddings(dve, it)
                                    if q == 4:
                                        dve.wait_ge(root_multiplied, it + 1)
                                        nc.vector.tensor_tensor(root_sum[0:RN, :], root_psum[0:RN, :], B1[0:RN, :], ALU.add).then_inc(root_made, 1)
                                add(S - 1)
                    sig.clear()

        def second_pass():
            with ExitStack() as phase:
                sig = Signals(nc, phase)
                src_in, dst_in, rows_in, emb_in, weights_stored = (
                    sig.slots(n) for n in ("src_in", "dst_in", "rows_in", "emb_in", "weights_stored"))
                groups_begun = sig.one("groups_begun")
                moved, addressed, onehot_made, summed, window_added = sig.some(
                    "moved", "addressed", "onehot_made", "summed", "window_added")
                weights_seen, pre1, hidden1_made, pre2, hidden2_made, weights_multiplied, weights_made = sig.some(
                    "weights_seen", "pre1", "hidden1_made", "pre2", "hidden2_made", "weights_multiplied", "weights_made")
                root_in, root_turned, root_copied, root_multiplied, residual_made, residual_biased, root_made, root_stored = sig.some(
                    "root_in", "root_turned", "root_copied", "root_multiplied", "residual_made", "residual_biased", "root_made", "root_stored")
                hidden1, hidden2 = work[:, 0, 0:PAIRS * P], work[:, 1, 0:PAIRS * P]
                sums = [bank[q % 3][:, 0:W] for q in range(S)]
                psum_1, psum_2 = bank[3][:, 0:PAIRS * P], bank[4][:, 0:PAIRS * P]
                psum_w = [bank[5], bank[6]]

                start_rounds()
                with nc.Fori(0, span + 1, W):
                    with nc.Block() as block:
                        @block.sync
                        def _(sp):
                            def load(it, q):
                                sp.wait_ge(summed, it * S + (q + 1))
                                load_indices(sp, q, it * S + q, src_in, dst_in)
                                sp.dma_start(embT[:, q, :], group_of(emb_tab, it * S + q)).then_inc(emb_in[q], 16)
                                if q == 4:
                                    sp.wait_ge(root_made, it + 1)
                                    for to, tab in ((root_x, x), (root_h, h_tab), (root_o, o_tab)):
                                        sp.dma_start(to[0:RN, :], root_rows(tab, it)).then_inc(root_in, 16)

                            def store(it, q):
                                sp.wait_ge(weights_made, it * S + (q + 1))
                                sp.sem_inc(weights_seen, 1)
                                sp.dma_start(group_of(weight_tab, it * S + q), path_w[:, q, :]).then_inc(weights_stored[q], 16)
                                if q == 4:
                                    sp.wait_ge(root_made, it + 2)
                                    sp.sem_inc(weights_seen, 1)
                                    sp.dma_start(root_rows(root2_tab, it), root_sum[0:RN, :]).then_inc(root_stored, 16)

                            sp.sem_inc(root_turned, 1)
                            sp.sem_inc(root_made, 1)
                            for q in range(S):
                                load(0, q)
                            with sp.Fori(1, ITERS) as it:
                                for q in range(S):
                                    load(it, q)
                                    store(it - 1, q)
                            for q in range(S):
                                store(ITERS - 1, q)
                            for q in range(S):
                                sp.wait_ge(weights_stored[q], 16 * ITERS)
                            sp.wait_ge(root_stored, 16 * ITERS)

                        @block.gpsimd
                        def _(pool):
                            gather_rows(pool, o_tab, src_in, rows_in, groups_begun)

                        @block.tensor
                        def _(pe):
                            pe.sem_inc(summed, S)

                            def add_tiles(q, tiles):
                                for t in tiles:
                                    last = nc.tensor.matmul(sums[q], gathered[:, q, D * t:D * (t + 1)], onehot[:, q, t, :],
                                                            start=(t == 0), stop=(t == T - 1))
                                return last

                            def step(it, q, first=False):
                                pe.wait_ge(emb_in[q], it * 16 + 16)
                                for j in range(PAIRS):
                                    last = nc.tensor.matmul(psum_1[:, P * j:P * (j + 1)], M0[:, j, :], embT[:, q, :], start=True, stop=True)
                                last.then_inc(pre1, 1)
                                pe.wait_ge(onehot_made, it * S + (q + 1))
                                if not (first and q < 2):
                                    pe.wait_ge(window_added, it * S + (q - 1))
                                pe.wait_ge(rows_in[q], it * 16 * T + 16 * T)
                                add_tiles(q, range(3))
                                pe.wait_ge(hidden1_made, it * S + (q + 1))
                                nc.tensor.matmul(psum_2, M1[:, :], hidden1, start=True, stop=True).then_inc(pre2, 1)
                                add_tiles(q, range(3, T)).then_inc(summed, 1)
                                if not (first and q == 0):
                                    pe.wait_ge(weights_made, it * S + q)
                                pe.wait_ge(hidden2_made, it * S + (q + 1))
                                for j in range(PAIRS):
                                    n = min(2, T - 2 * j) * D
                                    to = psum_w[j // 2][:, 2 * D * (j % 2):2 * D * (j % 2) + n]
                                    last = nc.tensor.matmul(to, hidden2[:, P * j:P * (j + 1)], M2[:, 0:n], start=True, stop=True)
                                last.then_inc(weights_multiplied, 1)
                                if q == 1:
                                    turn_root_rows(pe, it, root_o, root_in, 48, root_made, root_turned)
                                if q == 2:
                                    root_product(pe, it, W2R, root_copied, root_multiplied)

                            for q in range(S):
                                step(0, q, first=True)
                            with pe.Fori(1, ITERS) as it:
                                for q in range(S):
                                    step(it, q)

                        @block.scalar
                        def _(act):
                            with act.Fori(0, ITERS) as it:
                                for q in range(S):
                                    act.wait_ge(pre1, it * S + (q + 1))
                                    nc.scalar.activation(hidden1, psum_1, ACT.Silu, bias=MB0[:, :]).then_inc(hidden1_made, 1)
                                    act.wait_ge(pre2, it * S + (q + 1))
                                    nc.scalar.activation(hidden2, psum_2, ACT.Silu, bias=MB1[:, :]).then_inc(hidden2_made, 1)
                                    if q == 1:
                                        copy_root_columns(act, it, root_turned, root_copied)

                        @block.vector
                        def _(dve):
                            move_windows(dve, moved, addressed)

                            def make(it, q):
                                dve.wait_ge(dst_in[q], it * 16 + 16)
                                make_onehot(q, it * S + q).then_inc(onehot_made, 1)

                            def add(it, q):
                                dve.wait_ge(summed, it * S + (q + 1 + S))
                                add_window(dve, it * S + q, 1, sums[q]).then_inc(window_added, 1)
                                dve.wait_ge(window_added, it * S + (q + 1))

                            def keep_weights(it, q, reused):
                                dve.wait_ge(weights_multiplied, it * S + (q + 1))
                                if reused:
                                    dve.wait_ge(weights_stored[q], it * 16)
                                nc.vector.tensor_tensor(path_w[:, q, 0:4 * D].rearrange("p (t d) -> p t d", t=4),
                                                        psum_w[0][:, :].rearrange("p (t d) -> p t d", t=4),
                                                        spread(MB2[:, :].rearrange("p (a d) -> p a d", a=1), [P, 4, D]), ALU.add)
                                nc.vector.tensor_tensor(path_w[:, q, 4 * D:T * D], psum_w[1][:, 0:D], MB2[:, :], ALU.add).then_inc(weights_made, 1)

                            def root_terms(it, reused):
                                dve.wait_ge(root_in, it * 48 + 48)
                                if reused:
                                    dve.wait_ge(root_stored, it * 16)
                                to = root_sum[0:RN, :]
                                nc.vector.tensor_tensor(to, root_x[0:RN, :], root_h[0:RN, :], ALU.add).then_inc(residual_made, 1)
                                dve.wait_ge(residual_made, it + 1)
                                nc.vector.tensor_tensor(to, to, B2[0:RN, :], ALU.add).then_inc(residual_biased, 1)
                                dve.wait_ge(residual_biased, it + 1)
                                dve.wait_ge(root_multiplied, it + 1)
                                nc.vector.tensor_tensor(to, root_psum[0:RN, :], to, ALU.add).then_inc(root_made, 1)

                            def steps(it, first=False, last=False):
                                for q in range(S):
                                    if q < S - 1:
                                        make(it, q + 1)
                                    elif not last:
                                        make(it + 1, 0)
                                    if q >= 1:
                                        add(it, q - 1)
                                    elif not first:
                                        add(it - 1, S - 1)
                                    keep_weights(it, q, not first)
                                    if q == 3:
                                        root_terms(it, not first)

                            make(0, 0)
                            steps(0, first=True)
                            if ITERS > 2:
                                with dve.Fori(1, ITERS - 1) as it:
                                    steps(it)
                            steps(ITERS - 1, last=True)
                            add(ITERS - 1, S - 1)
                    sig.clear()

        def message_pass():
            with ExitStack() as phase:
                sig = Signals(nc, phase)
                src_in, dst_in, rows_in, dirs_in, weights_in = (
                    sig.slots(n) for n in ("src_in", "dst_in", "rows_in", "dirs_in", "weights_in"))
                groups_begun = sig.one("groups_begun")
                moved, addressed, onehot_made, summed, window_added = sig.some(
                    "moved", "addressed", "onehot_made", "summed", "window_added")
                scalar_made, product_made, dot_step, dot_made, msgs_made = sig.some(
                    "scalar_made", "product_made", "dot_step", "dot_made", "msgs_made")
                sums = [bank[q][:, 0:2 * W] for q in range(S)]

                start_rounds()
                with nc.Fori(0, span + 1, W):
                    with nc.Block() as block:
                        @block.sync
                        def _(sp):
                            with sp.Fori(0, ITERS) as it:
                                for q in range(S):
                                    sp.wait_ge(summed, it * S + (q + 1))
                                    g = it * S + q
                                    load_indices(sp, q, g, src_in, dst_in)
                                    sp.dma_start(dirs[:, q, :], group_of(dir_tab, g)).then_inc(dirs_in[q], 16)
                                    sp.dma_start(path_w[:, q, :], group_of(weight_tab, g)).then_inc(weights_in[q], 16)

                        @block.gpsimd
                        def _(pool):
                            gather_rows(pool, up_tab, src_in, rows_in, groups_begun)

                        @block.tensor
                        def _(pe):
                            pe.sem_inc(summed, S)
                            with pe.Fori(0, ITERS) as it:
                                for q in range(S):
                                    pe.wait_ge(msgs_made, it * S + (q + 1))
                                    for half in range(2):
                                        for t in range(T):
                                            last = nc.tensor.matmul(sums[q][:, W * half:W * (half + 1)],
                                                                    msgs[:, q, 2 * D * t + D * half:2 * D * t + D * (half + 1)],
                                                                    onehot[:, q, t, :], start=(t == 0), stop=(t == T - 1))
                                    last.then_inc(summed, 1)

                        @block.vector
                        def _(dve):
                            dve.sem_inc(window_added, 1)
                            move_windows(dve, moved, addressed)

                            def add(it, q):
                                dve.wait_ge(summed, it * S + (q + 1 + S))
                                dve.wait_ge(window_added, it * S + (q + 1))
                                add_window(dve, it * S + q, 2, sums[q]).then_inc(window_added, 1)

                            def step(it, q):
                                n = it * S + (q + 1)
                                row = gathered[:, q, :].rearrange("p (t f) -> p t f", t=T)
                                s_row = row[:, :, 0:MUL]
                                v_row = row[:, :, MUL:D].rearrange("p t (c k) -> p t c k", c=3)
                                w = path_w[:, q, :].rearrange("p (t j k) -> p t j k", t=T, j=4)
                                m = msgs[:, q, :].rearrange("p (t j k) -> p t j k", t=T, j=8)
                                m3 = m[:, :, 1, :]
                                m1 = m[:, :, 2:8:2, :]
                                m2 = m[:, :, 3:8:2, :]
                                y = spread(dirs[:, q, :].rearrange("p (t c a) -> p t c a", t=T, a=1), [P, T, 3, MUL])

                                def thrice(ap):
                                    return spread(ap.rearrange("p t (a k) -> p t a k", a=1), [P, T, 3, MUL])

                                dve.wait_ge(dst_in[q], it * 16 + 16)
                                make_onehot(q, it * S + q).then_inc(onehot_made, 1)
                                dve.wait_ge(dirs_in[q], it * 16 + 16)
                                dve.wait_ge(rows_in[q], it * 16 * T + 16 * T)
                                nc.vector.tensor_tensor(m1, v_row, y, ALU.mult).then_inc(product_made, 1)
                                dve.wait_ge(weights_in[q], it * 16 + 16)
                                nc.vector.tensor_tensor(w[:, :, 1, :], w[:, :, 1, :], s_row, ALU.mult).then_inc(scalar_made, 1)
                                dve.wait_ge(product_made, n)
                                nc.vector.tensor_tensor(m3, m1[:, :, 0, :], m1[:, :, 1, :], ALU.add).then_inc(dot_step, 1)
                                nc.vector.tensor_tensor(m[:, :, 0, :], w[:, :, 0, :], s_row, ALU.mult)
                                dve.wait_ge(dot_step, n)
                                nc.vector.tensor_tensor(m3, m3, m1[:, :, 2, :], ALU.add).then_inc(dot_made, 1)
                                nc.vector.tensor_tensor(m2, thrice(w[:, :, 2, :]), v_row, ALU.mult)
                                dve.wait_ge(scalar_made, n)
                                dve.wait_ge(dot_made, n)
                                nc.vector.tensor_tensor(m1, thrice(w[:, :, 1, :]), y, ALU.mult)
                                nc.vector.scalar_tensor_tensor(out=m3, in0=m3, scalar=1.0 / math.sqrt(3.0), in1=w[:, :, 3, :],
                                                               op0=ALU.mult, op1=ALU.mult).then_inc(msgs_made, 1)

                            def steps(it, first=False):
                                for q in range(S):
                                    step(it, q)
                                    if q >= 2:
                                        add(it, q - 2)
                                    elif not first:
                                        add(it - 1, q + S - 2)

                            steps(0, first=True)
                            with dve.Fori(1, ITERS) as it:
                                steps(it)
                            for q in (S - 2, S - 1):
                                add(ITERS - 1, q)
                    sig.clear()

        def first_hop():
            with ExitStack() as phase:
                sig = Signals(nc, phase)
                root_in, o_stored = sig.slots("root_in"), sig.slots("o_stored")
                waited, pool_waited, sums_copied, degs_copied, degs_turned, degs_kept, degs_inverted = sig.some(
                    "waited", "pool_waited", "sums_copied", "degs_copied", "degs_turned", "degs_kept", "degs_inverted")
                act_waited, product_made, pre_made, o_made, o_free = sig.some("act_waited", "product_made", "pre_made", "o_made", "o_free")
                with nc.Block() as block:
                    @block.sync
                    def _(sp):
                        sp.sem_inc(pre_made, S)
                        with sp.Fori(0, CITERS) as it:
                            for q in range(S):
                                sp.wait_ge(pre_made, it * S + (q + 1))
                                sp.dma_start(slot_a[q], chunk_of(root1_tab, it * S + q)).then_inc(root_in[q], 16)

                    @block.vector
                    def _(dve):
                        def copy_degs(it, q):
                            nc.vector.tensor_copy(slot_deg[q], agg[0:1, 1, ds((it * S + q) * CH, CH)]).then_inc(degs_copied, 1)

                        def finish(it, q):
                            s, c = it * S + (q + 1), it * S + q
                            dve.wait_ge(degs_turned, s)
                            degs = inv_deg[:, ds(c * NK, NK)]
                            nc.vector.tensor_scalar(degs, bank[5 + q % 3][0:NR, 0:NK], 1.0, None, ALU.max).then_inc(degs_kept, 1)
                            dve.wait_ge(degs_kept, it * S + (q + 3))
                            dve.sem_inc(waited, 1)
                            nc.vector.reciprocal(degs, degs).then_inc(degs_inverted, 1)
                            dve.wait_ge(degs_inverted, s)
                            dve.wait_ge(product_made, s)
                            dve.wait_ge(root_in[q], it * 16 + 16)
                            dve.wait_ge(o_free, s)
                            scaled_plus(slot_b[q], bank[q], c, slot_a[q]).then_inc(pre_made, 1)

                        dve.sem_inc(degs_kept, 2)
                        chunk_steps(dve, (0, copy_degs), (1, finish))

                    @block.tensor
                    def _(pe):
                        with pe.Fori(0, CITERS) as it:
                            for q in range(S):
                                pe.wait_ge(degs_copied, it * S + (q + 1))
                                pe.wait_ge(degs_kept, it * S + (q + 1))
                                for k in range(NK):
                                    last = nc.tensor.matmul(bank[5 + q % 3][0:NR, k:k + 1], strided(slot_deg[q])(k), ones[0:1, 0:1],
                                                            start=True, stop=True)
                                last.then_inc(degs_turned, 1)
                                pe.wait_ge(sums_copied, it * S + (q + 1))
                                row_matmuls(bank[q], [(strided(slot_sum[q]), W1L)]).then_inc(product_made, 1)

                    @block.scalar
                    def _(act):
                        def take_sums(it, q):
                            cols = ds((it * S + q) * CH, CH)
                            nc.scalar.activation(slot_sum[q], agg[:, 0, cols], ACT.Copy).then_inc(sums_copied, 1)
                            act.wait_ge(sums_copied, it * S + (q + 1))
                            act.sem_inc(act_waited, 1)
                            nc.scalar.activation(agg[:, 0, cols], zeros[:, :], ACT.Copy)
                            act.wait_ge(degs_copied, it * S + (q + 1))
                            act.sem_inc(act_waited, 1)
                            nc.scalar.activation(agg[:, 1, cols], zeros[:, :], ACT.Copy)

                        def relu(it, q):
                            act.wait_ge(pre_made, it * S + (q + 1 + S))
                            nc.scalar.activation(slot_b[q], slot_b[q], ACT.Relu).then_inc(o_made, 1)

                        act.sem_inc(o_free, S)
                        act.sem_inc(o_made, S)
                        chunk_steps(act, (0, take_sums), (1, relu))
                        for half in range(2):
                            nc.scalar.activation(agg[:, half, N:N + W], zeros[:, 0:W], ACT.Copy)

                    @block.gpsimd
                    def _(pool):
                        store_chunks(pool, o_tab, slot_b, o_made, o_stored, o_free, pool_waited)
                sig.clear()

        def second_hop():
            with ExitStack() as phase:
                sig = Signals(nc, phase)
                root_in, x2_stored, up_stored = (sig.slots(n) for n in ("root_in", "x2_stored", "up_stored"))
                sums_copied, product_made, x2_made, x2_free, normed, normed_turned, normed_copied = sig.some(
                    "sums_copied", "product_made", "x2_made", "x2_free", "normed", "normed_turned", "normed_copied")
                waited, act_waited, pool_waited, stats_made, var_made, std_made, inverted, up_made, up_copied, up_free = sig.some(
                    "waited", "act_waited", "pool_waited", "stats_made", "var_made", "std_made", "inverted", "up_made", "up_copied", "up_free")
                with nc.Block() as block:
                    @block.sync
                    def _(sp):
                        sp.sem_inc(normed_turned, S)
                        with sp.Fori(0, CITERS) as it:
                            for q in range(S):
                                sp.wait_ge(normed_turned, it * S + (q + 1))
                                sp.dma_start(slot_a[q], chunk_of(root2_tab, it * S + q)).then_inc(root_in[q], 16)

                    @block.scalar
                    def _(act):
                        def take_sums(it, q):
                            cols = ds((it * S + q) * CH, CH)
                            nc.scalar.activation(slot_sum[q], agg[:, 0, cols], ACT.Copy).then_inc(sums_copied, 1)
                            act.wait_ge(sums_copied, it * S + (q + 1))
                            act.sem_inc(act_waited, 1)
                            nc.scalar.activation(agg[:, 0, cols], zeros[:, :], ACT.Copy)

                        def std(it, q):
                            act.wait_ge(var_made, it * S + (q + 1))
                            row_std(q).then_inc(std_made, 1)

                        def relu_columns(it, q):
                            act.wait_ge(normed_turned, it * S + (q + 1 + S))
                            nc.scalar.activation(slot_t[q], bank[3][:, 0:CH], ACT.Relu).then_inc(normed_copied, 1)

                        def copy_up(it, q):
                            act.wait_ge(up_made, it * S + (q + 1))
                            act.wait_ge(up_free, it * S + (q + 1))
                            nc.scalar.activation(slot_c[q], rows_of(bank[4]), ACT.Copy, scale=1.0 / math.sqrt(MUL)).then_inc(up_copied, 1)

                        act.sem_inc(normed_copied, 1)
                        act.sem_inc(up_copied, 1)
                        chunk_steps(act, (0, take_sums), (1, std), (2, relu_columns), (3, copy_up))
                        nc.scalar.activation(agg[:, 0, N:N + W], zeros[:, 0:W], ACT.Copy)

                    @block.tensor
                    def _(pe):
                        def product(it, q):
                            pe.wait_ge(sums_copied, it * S + (q + 1))
                            pe.wait_ge(x2_made, it * S + (q + 1))
                            row_matmuls(bank[q % 3], [(strided(slot_sum[q]), W2L)]).then_inc(product_made, 1)

                        def turn(it, q):
                            pe.wait_ge(normed, it * S + (q + 1))
                            pe.wait_ge(normed_copied, it * S + (q + 1))
                            for k in range(NK):
                                last = nc.tensor.transpose(bank[3][:, NR * k:NR * (k + 1)], slot_a[q][:, k, :], ident[0:NR, 0:NR])
                            last.then_inc(normed_turned, 1)

                        def up(it, q):
                            pe.wait_ge(normed_copied, it * S + (q + 2))
                            pe.wait_ge(up_copied, it * S + (q + 1))
                            row_matmuls(bank[4], [(packed(slot_t[q]), WUP)]).then_inc(up_made, 1)

                        chunk_steps(pe, (0, product), (2, turn), (3, up))

                    @block.vector
                    def _(dve):
                        def x2(it, q):
                            s = it * S + (q + 1)
                            dve.wait_ge(root_in[q], it * 16 + 16)
                            dve.wait_ge(x2_free, s)
                            dve.wait_ge(product_made, s)
                            scaled_plus(slot_b[q], bank[q % 3], it * S + q, slot_a[q]).then_inc(x2_made, 1)
                            dve.wait_ge(x2_made, it * S + (q + 3))
                            row_stats(dve, q, slot_b[q], s, stats_made, var_made, waited)

                        def norm(it, q):
                            invert_std(dve, q, it * S + (q + 1), std_made, inverted)
                            for k in range(NK):
                                last = nc.vector.tensor_scalar(slot_a[q][:, k, :], slot_b[q][:, k, :], mean_var[0:NR, q, k, 0:1],
                                                               rstd[0:NR, q, k:k + 1], ALU.subtract, ALU.mult)
                            last.then_inc(normed, 1)

                        dve.sem_inc(x2_made, 2)
                        chunk_steps(dve, (0, x2), (1, norm))

                    @block.gpsimd
                    def _(pool):
                        def store_x2(it, q):
                            pool.wait_ge(x2_made, it * S + (q + 3))
                            pool.sem_inc(pool_waited, 1)
                            pool.dma_start(chunk_of(x2_tab, it * S + q), slot_b[q]).then_inc(x2_stored[q], 16)

                        def free_x2(it, q):
                            pool.wait_ge(x2_stored[q], it * 16 + 16)
                            pool.wait_ge(normed, it * S + (q + 1))
                            pool.sem_inc(x2_free, 1)

                        def store_up(it, q):
                            pool.wait_ge(up_copied, it * S + (q + 2))
                            pool.sem_inc(pool_waited, 1)
                            pool.dma_start(chunk_of(up_tab, it * S + q), slot_c[q]).then_inc(up_stored[q], 16)

                        def free_up(it, q):
                            pool.wait_ge(up_stored[q], it * 16 + 16)
                            pool.sem_inc(up_free, 1)

                        pool.sem_inc(x2_free, S)
                        pool.sem_inc(up_free, S)
                        chunk_steps(pool, (0, store_x2), (2, free_x2), (3, store_up), (4, free_up))
                        sig_reset(pool, x2_stored + up_stored)
                sig.clear()

        def output():
            with ExitStack() as phase:
                sig = Signals(nc, phase)
                x2_in, out_stored = sig.slots("x2_in"), sig.slots("out_stored")
                pool_waited = sig.one("pool_waited")
                sums_copied, product_made, out_made, out_free = sig.some("sums_copied", "product_made", "out_made", "out_free")
                with nc.Block() as block:
                    @block.sync
                    def _(sp):
                        sp.sem_inc(out_made, S)
                        with sp.Fori(0, CITERS) as it:
                            for q in range(S):
                                sp.wait_ge(out_made, it * S + (q + 1))
                                sp.dma_start(slot_a[q], chunk_of(x2_tab, it * S + q)).then_inc(x2_in[q], 16)

                    @block.scalar
                    def _(act):
                        with act.Fori(0, CITERS) as it:
                            for q in range(S):
                                cols = ds((it * S + q) * CH, CH)
                                act.wait_ge(out_made, it * S + (q + 1))
                                nc.scalar.activation(slot_sum[q], agg[:, 0, cols], ACT.Copy)
                                nc.scalar.activation(slot_t[q], agg[:, 1, cols], ACT.Copy).then_inc(sums_copied, 1)

                    @block.tensor
                    def _(pe):
                        with pe.Fori(0, CITERS) as it:
                            for q in range(S):
                                pe.wait_ge(sums_copied, it * S + (q + 1))
                                row_matmuls(bank[q], [(strided(slot_sum[q]), WOA), (strided(slot_t[q]), WOB)]).then_inc(product_made, 1)

                    @block.vector
                    def _(dve):
                        dve.sem_inc(out_free, S)
                        with dve.Fori(0, CITERS) as it:
                            for q in range(S):
                                dve.wait_ge(x2_in[q], it * 16 + 16)
                                dve.wait_ge(out_free, it * S + (q + 1))
                                dve.wait_ge(product_made, it * S + (q + 1))
                                nc.vector.scalar_tensor_tensor(
                                    out=slot_b[q].rearrange("p k d -> p (k d)"), in0=bank[q][0:NR, :],
                                    scalar=1.0 / (math.sqrt(2 * MUL) * AVG), in1=slot_a[q].rearrange("p k d -> p (k d)"),
                                    op0=ALU.mult, op1=ALU.add).then_inc(out_made, 1)

                    @block.gpsimd
                    def _(pool):
                        store_chunks(pool, out, slot_b, out_made, out_stored, out_free, pool_waited)
                sig.clear()

        first_pass()
        first_hop()
        second_pass()
        second_hop()
        message_pass()
        output()


INPUTS = ["x", "src", "dst", "edge_attr_3", "edge_weight",
          "L0_gnn_W1_l", "L0_gnn_W1_r", "L0_gnn_b1", "L0_gnn_W2_l", "L0_gnn_W2_r", "L0_gnn_b2",
          "L1_gnn_W_up0", "L1_gnn_W_up1", "L1_gnn_mlp_w0", "L1_gnn_mlp_b0", "L1_gnn_mlp_w1", "L1_gnn_mlp_b1",
          "L1_gnn_mlp_w2", "L1_gnn_mlp_b2", "L1_gnn_W_out0", "L1_gnn_W_out1"]


def kernel(**inputs):
    import numpy as np
    from concourse import bacc
    from concourse.bass_utils import run_bass_kernel_spmd

    nc = bacc.Bacc("TRN2", target_bir_lowering=False, num_devices=1)
    arrays, args = {}, []
    for name in INPUTS:
        a = np.ascontiguousarray(inputs[name])
        arrays[f"in_{name}"] = a
        args.append(nc.dram_tensor(f"in_{name}", a.shape, mybir.dt.from_np(a.dtype), kind="ExternalInput").ap())
    out = nc.dram_tensor("out", inputs["x"].shape, F32, kind="ExternalOutput").ap()
    program(nc, *args, out)
    r = run_bass_kernel_spmd(nc, [arrays], core_ids=[0])
    return r.results[0]["out"]
```
